# Optimizing a Trainium2 kernel written in Bass

```python
import numpy as np
import jax
import jax.numpy as jnp

def _softmax(x, axis=-1):
    return jax.nn.softmax(x, axis=axis)

def _gelu(x):
    return jax.nn.gelu(x, approximate=True)

def _silu(x):
    return jax.nn.silu(x)

def _sigmoid(x):
    return jax.nn.sigmoid(x)

def _layernorm(x, axis=-1, eps=1e-05):
    m = jnp.mean(x, axis=axis, keepdims=True)
    v = jnp.var(x, axis=axis, keepdims=True)
    return (x - m) / jnp.sqrt(v + eps)

def _scatter_add(tgt, idx, src, axis=0):
    return tgt.at[idx].add(src)

def _segment_sum(src, seg, n):
    return jax.ops.segment_sum(src, seg, n)
kernel_name = 'mk_gnn_resnorm_d2_gnn_r8_21c742'

def setup_inputs(seed: int=0):
    np.random.seed(seed)
    _w = jnp.asarray

    def _rec_inputs():
        import jax
        import jax.numpy as jnp
        _gk = jax.random.key(seed)
        x = -0.0003019 + 1 * jax.random.normal(jax.random.fold_in(_gk, 1), (2500, 1024), jnp.float32)
        src = jax.random.randint(jax.random.fold_in(_gk, 2), (80000,), 0, 2500, jnp.int32)
        dst = jnp.minimum((2500 * jax.random.uniform(jax.random.fold_in(_gk, 3), (80000,)) ** 2.0).astype(jnp.int32), 19999)
        _o = jnp.argsort(dst, stable=True)
        src = src[_o]
        dst = dst[_o]
        edge_weight = jax.random.uniform(jax.random.fold_in(_gk, 12), (80000,), jnp.float32, 0.0, 0.999998)
        return (x, src, dst, edge_weight)
    x, src, dst, edge_weight = _rec_inputs()

    def _L0_gnn_setup():
        import jax, jax.numpy as jnp
        import numpy as np
        N, IN_FEAT, OUT_FEAT, HEADS, E = (2500, 1024, 256, 4, 40000)
        NEG_SLOPE = 0.2
        key = jax.random.key(seed)
        k1, k2, k3, k4, k5, k6 = jax.random.split(key, 6)
        h = jax.random.normal(k1, (N, IN_FEAT), dtype=jnp.float32)
        src = jax.random.randint(k2, (E,), 0, N, dtype=jnp.int32)
        dst = jax.random.randint(k3, (E,), 0, N, dtype=jnp.int32)
        W = jax.random.normal(k4, (HEADS, IN_FEAT, OUT_FEAT), dtype=jnp.float32) * (1.0 / np.sqrt(IN_FEAT))
        a_l = jax.random.normal(k5, (HEADS, OUT_FEAT), dtype=jnp.float32) * (1.0 / np.sqrt(OUT_FEAT))
        a_r = jax.random.normal(k6, (HEADS, OUT_FEAT), dtype=jnp.float32) * (1.0 / np.sqrt(OUT_FEAT))
        return {'h': h, 'W': W, 'a_l': a_l, 'a_r': a_r, 'src': src, 'dst': dst}
    _L0_gnn_all = _L0_gnn_setup()
    _L0_gnn_in = {k: v for k, v in _L0_gnn_all.items() if k in ('W', 'a_l', 'a_r')}
    del _L0_gnn_all

    def _L1_gnn_setup():
        import jax, jax.numpy as jnp
        import numpy as np
        N_NODES = 2500
        N_EDGES = 40000
        F_IN = 1024
        F_OUT = 1024
        key = jax.random.key(seed)
        k1, k2, k3, k4, k5 = jax.random.split(key, 5)
        x = jax.random.normal(k1, (N_NODES, F_IN), dtype=jnp.float32)
        std = 1.0 / np.sqrt(F_OUT)
        W = jax.random.uniform(k2, (F_IN, F_OUT), minval=-std, maxval=std, dtype=jnp.float32)
        edge_w = jax.random.uniform(k3, (N_EDGES,), dtype=jnp.float32)
        src = jax.random.randint(k4, (N_EDGES,), 0, N_NODES, dtype=jnp.int32)
        dst = jax.random.randint(k5, (N_EDGES,), 0, N_NODES, dtype=jnp.int32)
        return {'x': x, 'W': W, 'edge_w': edge_w, 'src': src, 'dst': dst}
    _L1_gnn_all = _L1_gnn_setup()
    _L1_gnn_in = {k: v for k, v in _L1_gnn_all.items() if k in ('W',)}
    del _L1_gnn_all
    return {'x': x, 'src': src, 'dst': dst, 'edge_weight': edge_weight, 'L0_gnn_W': _L0_gnn_in['W'], 'L0_gnn_a_l': _L0_gnn_in['a_l'], 'L0_gnn_a_r': _L0_gnn_in['a_r'], 'L1_gnn_W': _L1_gnn_in['W']}

def reference(x, src, dst, edge_weight, L0_gnn_W, L0_gnn_a_l, L0_gnn_a_r, L1_gnn_W):
    import jax
    import jax.numpy as jnp

    def _L0_gnn_ref(h, W, a_l, a_r, src, dst):
        import jax, jax.numpy as jnp
        import numpy as np
        N, IN_FEAT, OUT_FEAT, HEADS, E = (2500, 1024, 256, 4, 40000)
        NEG_SLOPE = 0.2
        z = jnp.einsum('ni,hif->nhf', h, W)
        el = jnp.einsum('nhf,hf->nh', z, a_l)
        er = jnp.einsum('nhf,hf->nh', z, a_r)
        e = jax.nn.leaky_relu(el[src] + er[dst], NEG_SLOPE)
        m = jax.ops.segment_max(e, dst, num_segments=N)
        ex = jnp.exp(e - m[dst])
        s = jax.ops.segment_sum(ex, dst, num_segments=N)
        alpha = ex / s[dst]
        out = jax.ops.segment_sum(alpha[:, :, None] * z[src], dst, num_segments=N)
        return out.reshape(N, HEADS * OUT_FEAT)

    def _L1_gnn_ref(x, W, edge_w, src, dst):
        import jax, jax.numpy as jnp
        import numpy as np
        N_NODES = 2500
        N_EDGES = 40000
        F_IN = 1024
        F_OUT = 1024
        support = jnp.matmul(x, W)
        messages = support[src] * edge_w[:, None]
        out = jax.ops.segment_sum(messages, dst, num_segments=N_NODES)
        return out
    x = _layernorm(x + _L0_gnn_ref(x, L0_gnn_W, L0_gnn_a_l, L0_gnn_a_r, src, dst), axis=-1)
    x = _layernorm(x + _L1_gnn_ref(x, L1_gnn_W, edge_weight, src, dst), axis=-1)
    return x

_drawn_inputs = setup_inputs


def setup_inputs(seed=0):
    import zlib

    import numpy as np

    out = dict(_drawn_inputs(seed))
    spreads = {}
    factors = {}
    for name, (base, spread) in spreads.items():
        noise = np.random.default_rng([zlib.crc32(name.encode()), seed]).standard_normal(out[name].shape)
        drawn = base * np.exp(spread * noise) if base else spread * noise
        out[name] = jnp.asarray(drawn.astype(out[name].dtype))
    for name, factor in factors.items():
        out[name] = (out[name] * factor).astype(out[name].dtype)
    return out
```

```python
import concourse.bass as bass
from concourse import mybir
from contextlib import ExitStack


def gat_gcn_resnorm(nc, x, src, dst, edge_weight, W0, a_l, a_r, W1, out):
    f32, f32r = mybir.dt.float32, mybir.dt.float32r
    bf16, i32 = mybir.dt.bfloat16, mybir.dt.int32
    ALU, ACT, AX = mybir.AluOpType, mybir.ActivationFunctionType, mybir.AxisListType

    N, F = x.shape
    H, _, FH = W0.shape
    E = src.shape[0]
    T = 125
    NT = N // T
    KF = F // 128
    HALF = F // 2
    FA = FH + 1
    C = E // 128
    CB = C // T
    PAIRS = (C + 1) // 2
    CP = 2 * PAIRS
    WD = 25
    WC = WD * NT
    WT = T // WD
    NW = N // WD
    PARTS = 3
    R = PARTS * H
    BIG = 1.0e30
    ROUND = 12582912.0
    SLOPE = 0.2
    EPS = 1e-5
    FAR = -1.0e6
    assert N == NT * T and E == C * 128 and C == CB * T and NW <= 128 and WC <= 512

    w2_dram = nc.dram_tensor("w2_dram", (NT, T, NT * T), f32, kind="Internal").ap()
    x1_dram = nc.dram_tensor("x1_dram", (N, F), f32, kind="Internal").ap()
    range_dram = nc.dram_tensor("range_dram", (NW, 2), i32, kind="Internal").ap()
    x_t = x.rearrange("(t p) f -> t p f", p=T)
    x1_t = x1_dram.rearrange("(t p) f -> t p f", p=T)
    out_t = out.rearrange("(t p) f -> t p f", p=T)

    ctx = ExitStack()
    with ctx:
        def sb(name, shape, dt=f32):
            return ctx.enter_context(nc.sbuf_tensor(name, shape, dt))

        def sem(name):
            return ctx.enter_context(nc.semaphore(name))

        feats = sb("feats", [128, NT * H * FA])
        z = feats[0:T, :].rearrange("p (t h f) -> p t h f", t=NT, h=H)
        sup = feats[0:T, 0:NT * F].rearrange("p (t f) -> p t f", t=NT)
        wide = sb("wide", [128, 4 * NT * T])
        wmat = wide[:, 0:KF * F].rearrange("p (k f) -> p k f", k=KF)
        count = wide[0:T, 0:NT * T].rearrange("p (s d) -> p s d", s=NT)
        wsum = wide[0:T, NT * T:2 * NT * T].rearrange("p (s d) -> p s d", s=NT)
        absent = wide[0:T, 2 * NT * T:3 * NT * T].rearrange("p (s d) -> p s d", s=NT)
        reach = wide[0:T, 3 * NT * T:4 * NT * T].rearrange("p (s d) -> p s d", s=NT)
        w2buf = [wide[0:T, q * NT * T:(q + 1) * NT * T].rearrange("p (s d) -> p s d", s=NT) for q in range(2)]
        work = sb("work", [128, 6 * F])
        xt = [work[0:T, q * F:(q + 1) * F] for q in range(2)]
        xT = [work[:, (2 + q) * F:(2 + q) * F + KF * T].rearrange("p (k n) -> p k n", k=KF) for q in range(2)]
        acol = [work[:, (4 + q) * F:(5 + q) * F] for q in range(2)]
        xres = work[0:T, 0:F]
        xsum = work[0:T, F:2 * F]
        xnew = work[0:T, 2 * F:3 * F]
        prod = wide[:, KF * F:(KF + 1) * F]
        edge = wide[0:T, 0:10 * CB * 128].rearrange("p (a b k) -> p a b k", a=10, b=CB)
        EB = CB * 128
        raw_i = feats[:, 0:2 * EB].bitcast(i32).rearrange("p (a b k) -> p a b k", a=2, b=CB)
        whi_r = feats[:, 2 * EB:3 * EB].bitcast(f32r).rearrange("p (b k) -> p b k", b=CB)
        diag = feats[:, 3 * EB:3 * EB + 2 * CB * T].rearrange("p (a n) -> p a n", n=T)
        hit = feats[:, 6 * EB:6 * EB + 3 * C].rearrange("p (a c) -> p a c", a=3)
        key = sb("key", [128, CP])
        low = sb("low", [128, CP])
        weight_hi = sb("weight_hi", [128, CP])
        weight_lo = sb("weight_lo", [128, CP])
        ident = sb("ident", [128, 128])
        ident_b = sb("ident_b", [128, 128], bf16)
        ones = sb("ones", [128, 128])
        iota_i = sb("iota_i", [128, CB * 128], i32)
        iota = sb("iota", [128, CB * 128])
        lane_i = sb("lane_i", [128, 1], i32)
        lane = sb("lane", [128, 1])
        span = sb("span", [128, 2, CB])
        rng = sb("rng", [128, 8])
        rng_i = sb("rng_i", [128, 2], i32)
        ranges = sb("ranges", [1, NW * 2], i32)
        zeros = sb("zeros", [128, 512], f32r)
        onehot_d = [sb(f"onehot_d{j}", [128, WC], f32r) for j in range(2)]
        onehot_s = [sb(f"onehot_s{j}", [128, T], f32r) for j in range(2)]
        weighted = [sb(f"weighted{j}", [128, 2, T], f32r) for j in range(2)]
        wa = sb("wa", [128, KF, 2 * H])
        elr = sb("elr", [128, NT, 2 * H])
        part_f = sb("part_f", [128, NT, 2, H])
        elc = sb("elc", [128, NT, 2, 2 * R], bf16)
        lrow = sb("lrow", [128, NT, 2, T], bf16)
        block_mask = sb("block_mask", [128, H, T], bf16)
        peak = sb("peak", [128, H, T])
        small = sb("small", [128, 12, H])
        q = sb("q", [128, 2, H])
        q_left = sb("q_left", [128, 2, H])
        qc = sb("qc", [128, 2, 2 * R], bf16)
        qrow = sb("qrow", [128, 2, H, T], bf16)
        e_pos = [sb(f"e_pos{j}", [128, H * T]) for j in range(2)]
        e_neg = [sb(f"e_neg{j}", [128, H * T]) for j in range(2)]
        e_max = [sb(f"e_max{j}", [128, H * T]) for j in range(2)]
        prob = [sb(f"prob{j}", [128, H, T]) for j in range(4)]
        stats = sb("stats", [128, 2, 6])
        moments = sb("moments", [128, 2])
        spread = sb("spread", [128, 3])

        ps = ctx.enter_context(nc.psum_tensor("ps", [128, 8, 512], f32))
        def bf_view(bank):
            return ps[:, bank, :].bitcast(bf16)

        names = """edges_in weights_in attn_in w1_in const_made const_self range_out range_in
            edge_made edge_turned edge_kept diag_made range_spread vec_made
            x0_in x1_in turned xT_made xT_act product z_kept z_kept_act elc_made el_turned lrow_made
            made0 made1 weighted0 weighted1 used0 used1 c_kept w_kept wsum_free w2_out
            peak_made peak_turned q_made q_turned qrow_made scores exp_done emax_done prob_done
            agg_done agg_kept res_in res_free var_made std_made x1_made x1_out x1_free
            chain
            l1_x0_in l1_x1_in l1_turned l1_xT_made l1_xT_act l1_product l1_kept l1_kept_act
            w2_in0 w2_in1 l1_agg l1_agg_kept l1_res_in l1_var l1_std l1_made l1_out l1_free
            l1_w1_in""".split()
        S = {n: sem(n) for n in names}
        made, used, weighted_made = [S["made0"], S["made1"]], [S["used0"], S["used1"]], [S["weighted0"], S["weighted1"]]

        block = ctx.enter_context(nc.Block())

        @block.sync
        def _(sp):
            sp.dma_start(raw_i[0:T, 0], src.rearrange("(b r k) -> r b k", b=CB, r=T)).then_inc(S["edges_in"], 16)
            sp.dma_start(raw_i[0:T, 1], dst.rearrange("(b r k) -> r b k", b=CB, r=T)).then_inc(S["edges_in"], 16)
            sp.dma_start(edge[:, 0], edge_weight.rearrange("(b r k) -> r b k", b=CB, r=T)).then_inc(S["edges_in"], 16)
            sp.wait_ge(S["range_out"], 1)
            sp.dma_start(range_dram, rng_i[0:NW, :]).then_inc(S["range_in"], 16)
            sp.wait_ge(S["range_in"], 16)
            sp.dma_start(ranges[:, :], range_dram.rearrange("(o w) r -> o (w r)", o=1)).then_inc(S["range_in"], 16)
            for h in range(H):
                sp.dma_start(wmat[:, :, h * FH:(h + 1) * FH],
                             W0[h].rearrange("(k p) f -> p k f", p=128)).then_inc(S["weights_in"], 16)
            for n, a in enumerate((a_l, a_r)):
                sp.dma_start(acol[n], a.rearrange("(o h) f -> o (h f)", o=1).to_broadcast([128, F])).then_inc(S["attn_in"], 16)
            with sp.Fori(0, NT // 2) as i:
                for b, arrived in enumerate((S["x0_in"], S["x1_in"])):
                    sp.wait_ge(S["turned"], 2 * i + b + 1)
                    sp.dma_start(xt[b], x_t[bass.ds(2 * i + b, 1)].rearrange("o p f -> (o p) f")).then_inc(arrived, 16)
            sp.wait_ge(S["z_kept"], NT)
            sp.sem_inc(S["wsum_free"], 1)
            sp.sem_inc(S["x1_free"], 1)
            with sp.Fori(0, NT) as t:
                sp.wait_ge(S["res_free"], t + 1)
                sp.dma_start(xres, x_t[bass.ds(t, 1)].rearrange("o p f -> (o p) f")).then_inc(S["res_in"], 16)
                sp.wait_ge(S["w_kept"], WT * (t + 1) + 1)
                sp.dma_start(w2_dram[bass.ds(t, 1)].rearrange("o p f -> (o p) f"),
                             wide[0:T, NT * T:2 * NT * T]).then_inc(S["w2_out"], 16)
                sp.wait_ge(S["w2_out"], 16 * t + 16)
                sp.sem_inc(S["wsum_free"], 1)
                sp.wait_ge(S["x1_made"], t + 1)
                sp.dma_start(x1_t[bass.ds(t, 1)].rearrange("o p f -> (o p) f"), xnew).then_inc(S["x1_out"], 16)
                sp.wait_ge(S["x1_out"], 16 * t + 16)
                sp.sem_inc(S["x1_free"], 1)
            sp.dma_start(wmat, W1.rearrange("(k p) f -> p k f", p=128)).then_inc(S["l1_w1_in"], 16)
            with sp.Fori(0, NT // 2) as i:
                for b, arrived in enumerate((S["l1_x0_in"], S["l1_x1_in"])):
                    sp.wait_ge(S["l1_turned"], 2 * i + b + 1)
                    sp.dma_start(xt[b], x1_t[bass.ds(2 * i + b, 1)].rearrange("o p f -> (o p) f")).then_inc(arrived, 16)
            sp.wait_ge(S["l1_kept"], NT)
            with sp.Fori(0, NT // 2) as i:
                for b, arrived in enumerate((S["w2_in0"], S["w2_in1"])):
                    t = 2 * i + b
                    sp.wait_ge(S["l1_agg_kept"], t + 1)
                    sp.dma_start(wide[0:T, b * NT * T:(b + 1) * NT * T],
                                 w2_dram[bass.ds(t, 1)].rearrange("o p f -> (o p) f")).then_inc(arrived, 16)
                    sp.dma_start(xres if b == 0 else work[0:T, 3 * F:4 * F],
                                 x1_t[bass.ds(t, 1)].rearrange("o p f -> (o p) f")).then_inc(arrived, 16)
            sp.wait_ge(S["l1_out"], 16 * NT)

        @block.gpsimd
        def _(pool):
            n = [0]

            def link(ins):
                n[0] += 1
                ins.then_inc(S["const_self"], 1)
                pool.wait_ge(S["const_self"], n[0])

            link(pool.iota(iota_i[:], pattern=[[1, CB * 128]], base=0, channel_multiplier=0))
            link(pool.iota(lane_i[:], pattern=[[0, 1]], base=0, channel_multiplier=1))
            link(pool.tensor_copy(iota[:], iota_i[:]))
            link(pool.tensor_copy(lane[:], lane_i[:]))
            link(pool.memset(ident[:], 0.0))
            link(pool.affine_select(out=ident[:], in_=ident[:], compare_op=ALU.not_equal, fill=1.0,
                                    base=0, pattern=[[-1, 128]], channel_multiplier=1))
            link(pool.tensor_copy(ident_b[:], ident[:]))
            link(pool.memset(ones[:], 1.0))
            link(pool.memset(block_mask[:], 0.0))
            for j in range(2 * PARTS):
                link(pool.affine_select(out=block_mask[:], in_=block_mask[:], compare_op=ALU.not_equal, fill=1.0,
                                        base=-j * H, pattern=[[-1, H], [0, T]], channel_multiplier=1))
            link(pool.memset(elc[:], 1.0))
            link(pool.memset(lrow[:], 0.0))
            link(pool.memset(qrow[:], 0.0))
            pool.memset(qc[:], 1.0).then_inc(S["const_self"], 1)
            pool.wait_ge(S["const_self"], n[0] + 1)
            pool.sem_inc(S["const_made"], 1)

        def feature_product(pe, turned, xT_made, xT_act, product, arrived, attention):
            pe.sem_inc(turned, 2)
            with pe.Fori(0, NT // 2) as i:
                for b in range(2):
                    t = 2 * i + b
                    pe.wait_ge(arrived[b], 16 * i + 16)
                    for k in range(KF):
                        last = pe.transpose(ps[:, k // 4, (k % 4) * T:(k % 4 + 1) * T],
                                            xt[b][:, k * 128:(k + 1) * 128], ident[0:T, 0:T])
                    last.then_inc(turned, 1)
                    pe.wait_ge(xT_made, t + 1)
                    pe.wait_ge(xT_act, t + 1)
                    base = 2 + 3 * b
                    for n in range(2):
                        for k in range(KF):
                            last = pe.matmul(ps[0:T, base + n, :], xT[b][:, k, :],
                                             wmat[:, k, n * HALF:(n + 1) * HALF], start=(k == 0), stop=(k == KF - 1))
                    if attention:
                        for k in range(KF):
                            last = pe.matmul(ps[0:T, base + 2, 0:2 * H], xT[b][:, k, :], wa[:, k, :],
                                             start=(k == 0), stop=(k == KF - 1))
                    last.then_inc(product, 1)

        @block.tensor
        def _(pe):
            pe.wait_ge(S["const_made"], 1)
            pe.wait_ge(S["edge_made"], 1)
            for a in range(4):
                for b in range(CB):
                    last = pe.transpose(ps[:, 2 * a + b // 3, (b % 3) * T:(b % 3 + 1) * T], edge[:, 1 + a, b, :], ident[0:T, 0:T])
            last.then_inc(S["edge_turned"], 1)
            pe.wait_ge(S["edge_kept"], 1)
            pe.wait_ge(S["diag_made"], 1)
            for a in range(2):
                for b in range(CB):
                    last = pe.matmul(ps[0:T, 2 * a + b // 3, (b % 3) * T:(b % 3 + 1) * T], ones[0:T, 0:T],
                                     diag[0:T, a * CB + b, :], start=True, stop=True)
            last.then_inc(S["range_spread"], 1)
            pe.wait_ge(S["vec_made"], 1)
            feature_product(pe, S["turned"], S["xT_made"], S["xT_act"], S["product"],
                            (S["x0_in"], S["x1_in"]), True)
            pe.wait_ge(S["elc_made"], 1)
            pe.wait_ge(S["z_kept_act"], NT)
            for t in range(NT):
                for v in range(2):
                    n = 2 * t + v
                    last = pe.transpose(bf_view(n // 8)[0:2 * R, (n % 8) * 128:(n % 8) * 128 + T],
                                        elc[0:T, t, v, :], ident_b[0:T, 0:T])
            last.then_inc(S["el_turned"], 1)
            pe.wait_ge(S["lrow_made"], 1)

            for j in range(2):
                pe.sem_inc(used[j], 1)
            pe.sem_inc(S["agg_done"], 4)
            pe.wait_ge(S["range_in"], 32)
            step = pe.alloc_register("pe_step")
            pe.reg_mov(step, 0)
            with pe.Fori(0, NT) as t:
                bounds = []
                for w in range(WT):
                    bounds.append((pe.value_load(ranges[0:1, bass.ds(2 * WT * t + 2 * w, 1)], min_val=0, max_val=PAIRS - 1),
                                   pe.value_load(ranges[0:1, bass.ds(2 * WT * t + 2 * w + 1, 1)], min_val=1, max_val=PAIRS)))
                pe.wait_ge(S["exp_done"], NT * t + 1)
                for w in range(WT):
                    cb, wb = 4 + 2 * (w % 2), 5 + 2 * (w % 2)
                    pe.wait_ge(S["c_kept"], WT * t + max(0, w - 1) + 1)
                    pe.wait_ge(S["w_kept"], WT * t + max(0, w - 1) + 1)
                    for bank in (cb, wb):
                        pe.matmul(ps[0:T, bank, 0:WC], zeros[0:1, 0:T], zeros[0:1, 0:WC], start=True, stop=False,
                                  skip_group_check=True)
                    with pe.Fori(*bounds[w]) as g:
                        n = pe.snap(step, min_val=0, max_val=NW * PAIRS)
                        for j in range(2):
                            pe.wait_ge(made[j], n + 1)
                            pe.matmul(ps[0:T, cb, 0:WC], onehot_s[j][:, :], onehot_d[j][:, :], start=False, stop=True,
                                      skip_group_check=True)
                            pe.wait_ge(weighted_made[j], n + 1)
                            pe.matmul(ps[0:T, wb, 0:WC], weighted[j][:, 0, :], onehot_d[j][:, :], start=False, stop=True,
                                      skip_group_check=True)
                            pe.matmul(ps[0:T, wb, 0:WC], weighted[j][:, 1, :], onehot_d[j][:, :], start=False, stop=True,
                                      skip_group_check=True).then_inc(used[j], 1)
                        pe.reg_add(step, step, 1)
                pe.wait_ge(S["peak_made"], t + 1)
                pe.wait_ge(S["w_kept"], WT * t + WT + 1)
                for h in range(H):
                    last = pe.transpose(ps[0:T, 4, h * T:(h + 1) * T], peak[0:T, h, :], ident[0:T, 0:T])
                last.then_inc(S["peak_turned"], 1)
                pe.wait_ge(S["q_made"], t + 1)
                for v in range(2):
                    last = pe.transpose(bf_view(5)[0:2 * R, v * 128:v * 128 + T], qc[0:T, v, :], ident_b[0:T, 0:T])
                last.then_inc(S["q_turned"], 1)
                pe.wait_ge(S["qrow_made"], t + 1)

                def scores(s):
                    pe.wait_ge(S["exp_done"], NT * t + s + 1)
                    for v in range(2):
                        last = pe.matmul(ps[0:T, 6 + v, 0:H * T], lrow[:, bass.ds(s, 1), v, :].rearrange("p o n -> p (o n)"),
                                         qrow[:, v].rearrange("p h d -> p (h d)"), start=True, stop=True)
                    last.then_inc(S["scores"], 1)

                def group(s0, first, final):
                    for u in range(4):
                        s = s0 + u
                        if not (final and u == 3):
                            scores(s + 1)
                        pe.wait_ge(S["prob_done"], NT * t + s + 3)
                        for h in range(H):
                            last = pe.matmul(ps[0:T, h, 0:FA], prob[u][0:T, h, :],
                                             z[:, bass.ds(s, 1), h, :].rearrange("p o f -> p (o f)"),
                                             start=(first and u == 0), stop=(final and u == 3))
                        last.then_inc(S["agg_done"], 1)

                scores(0)
                pe.wait_ge(S["agg_kept"], t + 1)
                group(0, True, False)
                with pe.Fori(1, NT // 4 - 1) as g:
                    group(4 * g, False, False)
                group(NT - 4, False, True)

            pe.wait_ge(S["l1_w1_in"], 16)
            pe.wait_ge(S["agg_kept"], NT + 1)
            feature_product(pe, S["l1_turned"], S["l1_xT_made"], S["l1_xT_act"], S["l1_product"],
                            (S["l1_x0_in"], S["l1_x1_in"]), False)
            pe.wait_ge(S["l1_kept"], NT)
            pe.wait_ge(S["l1_kept_act"], NT)
            with pe.Fori(0, NT // 2) as i:
                for b, arrived in enumerate((S["w2_in0"], S["w2_in1"])):
                    t = 2 * i + b
                    pe.wait_ge(arrived, 32 * i + 32)
                    pe.wait_ge(S["l1_agg_kept"], t + 1)
                    for s in range(NT):
                        for n in range(2):
                            last = pe.matmul(ps[0:T, 2 * b + n, :], w2buf[b][:, s, :], sup[:, s, n * HALF:(n + 1) * HALF],
                                             start=(s == 0), stop=(s == NT - 1))
                    last.then_inc(S["l1_agg"], 1)

        def act_feature(act, turned, xT_act, product, kept_act, attention):
            with act.Fori(0, NT // 2) as i:
                for b in range(2):
                    t = 2 * i + b
                    act.wait_ge(turned, t + 3)
                    act.activation(xT[b][:, KF // 2:, :], ps[:, 1, 0:KF // 2 * T].rearrange("p (k n) -> p k n", k=KF // 2),
                                   ACT.Copy).then_inc(xT_act, 1)
                    act.wait_ge(product, t + 1)
                    base = 2 + 3 * b
                    if attention:
                        act.activation(z[:, bass.ds(t, 1), H // 2:, 0:FH].rearrange("p o h f -> p (o h) f"),
                                       ps[0:T, base + 1, :].rearrange("p (h f) -> p h f", h=H // 2), ACT.Copy).then_inc(kept_act, 1)
                    else:
                        act.activation(sup[:, bass.ds(t, 1), HALF:].rearrange("p o f -> p (o f)"),
                                       ps[0:T, base + 1, :], ACT.Copy).then_inc(kept_act, 1)

        @block.scalar
        def _(act):
            act_feature(act, S["turned"], S["xT_act"], S["product"], S["z_kept_act"], True)
            act.wait_ge(S["range_in"], 32)
            act.sem_inc(S["w_kept"], 1)
            act.sem_inc(S["exp_done"], 1)
            step = act.alloc_register("act_step")
            act.reg_mov(step, 0)
            with act.Fori(0, NT) as t:
                bounds = []
                for w in range(WT):
                    bounds.append((act.value_load(ranges[0:1, bass.ds(2 * WT * t + 2 * w, 1)], min_val=0, max_val=PAIRS - 1),
                                   act.value_load(ranges[0:1, bass.ds(2 * WT * t + 2 * w + 1, 1)], min_val=1, max_val=PAIRS)))
                for w in range(WT):
                    with act.Fori(*bounds[w]) as g:
                        n = act.snap(step, min_val=0, max_val=NW * PAIRS)
                        for j in range(2):
                            act.wait_ge(made[j], n + 1)
                            act.activation(weighted[j][:, 0, :], onehot_s[j][:, :].bitcast(f32), ACT.Copy,
                                           scale=weight_hi[:, bass.ds(2 * g + j, 1)])
                            act.activation(weighted[j][:, 1, :], onehot_s[j][:, :].bitcast(f32), ACT.Copy,
                                           scale=weight_lo[:, bass.ds(2 * g + j, 1)]).then_inc(weighted_made[j], 1)
                        act.reg_add(step, step, 1)
                    if w == 0:
                        act.wait_ge(S["wsum_free"], t + 1)
                    n = act.snap(step, min_val=0, max_val=NW * PAIRS)
                    act.wait_ge(used[1], n + 1)
                    act.activation(wsum[:, :, w * WD:(w + 1) * WD].rearrange("p s d -> p d s"),
                                   ps[0:T, 5 + 2 * (w % 2), 0:WC].rearrange("p (d s) -> p d s", d=WD),
                                   ACT.Copy).then_inc(S["w_kept"], 1)
                with act.Fori(0, NT // 2) as i:
                    for b in range(2):
                        s = NT * t + 2 * i + b
                        act.wait_ge(S["scores"], s + 1)
                        act.wait_ge(S["emax_done"], s + 1)
                        act.activation(e_pos[b][0:T], ps[0:T, 6, 0:H * T], ACT.Exp)
                        act.activation(e_neg[b][0:T], ps[0:T, 7, 0:H * T], ACT.Exp).then_inc(S["exp_done"], 1)
                act.wait_ge(S["var_made"], t + 1)
                act.activation(spread[0:T, 1:2], spread[0:T, 0:1], ACT.Sqrt).then_inc(S["std_made"], 1)
            act_feature(act, S["l1_turned"], S["l1_xT_act"], S["l1_product"], S["l1_kept_act"], False)
            act.sem_inc(S["l1_free"], 1)
            with act.Fori(0, NT) as t:
                act.wait_ge(S["l1_var"], t + 1)
                act.activation(spread[0:T, 1:2], spread[0:T, 0:1], ACT.Sqrt).then_inc(S["l1_std"], 1)
                act.wait_ge(S["l1_made"], t + 1)
                act.dma_start(out_t[bass.ds(t, 1)].rearrange("o p f -> (o p) f"), xnew).then_inc(S["l1_out"], 16)
                act.wait_ge(S["l1_out"], 16 * t + 16)
                act.sem_inc(S["l1_free"], 1)

        @block.vector
        def _(dve):
            n_chain = [0]

            def link(ins):
                n_chain[0] += 1
                ins.then_inc(S["chain"], 1)
                dve.wait_ge(S["chain"], n_chain[0])

            dve.wait_ge(S["edges_in"], 48)
            srcf, dstf, hi_s = edge[:, 5], edge[:, 6], edge[:, 7]
            e_low, e_key, e_whi, e_wlo, w_in = edge[:, 1], edge[:, 2], edge[:, 3], edge[:, 4], edge[:, 0]
            link(dve.tensor_copy(srcf, raw_i[0:T, 0]))
            link(dve.tensor_copy(dstf, raw_i[0:T, 1]))
            link(dve.tensor_scalar(hi_s, srcf, -(T // 2) * 1.0, 1.0 / T, ALU.add, ALU.mult))
            link(dve.tensor_scalar(hi_s, hi_s, ROUND, ROUND, ALU.add, ALU.subtract))
            link(dve.scalar_tensor_tensor(e_low, hi_s, -1.0 * T, srcf, ALU.mult, ALU.add))
            link(dve.scalar_tensor_tensor(e_key, dstf, 1.0 * NT, hi_s, ALU.mult, ALU.add))
            link(dve.tensor_copy(whi_r[0:T], w_in))
            link(dve.tensor_copy(e_whi, whi_r[0:T].bitcast(f32)))
            link(dve.tensor_tensor(e_wlo, w_in, e_whi, ALU.subtract))
            dve.sem_inc(S["edge_made"], 1)
            link(dve.tensor_reduce(span[0:T, 0], dstf, AX.X, ALU.min))
            link(dve.tensor_reduce(span[0:T, 1], dstf, AX.X, ALU.max))
            dve.wait_ge(S["const_made"], 1)
            for a in range(2):
                for b in range(CB):
                    link(dve.tensor_scalar(diag[0:T, a * CB + b, :], ident[0:T, 0:T], span[0:T, a, b:b + 1], None, ALU.mult))
            dve.sem_inc(S["diag_made"], 1)
            link(dve.memset(key[:, C:CP], FAR))
            link(dve.memset(low[:, C:CP], FAR))
            link(dve.memset(weight_hi[:, C:CP], 0.0))
            link(dve.memset(weight_lo[:, C:CP], 0.0))
            link(dve.memset(zeros[:].bitcast(f32), 0.0))
            dve.wait_ge(S["edge_turned"], 1)
            for a, to in enumerate((low, key, weight_hi, weight_lo)):
                for n in range(2):
                    width = min(3, CB - 3 * n) * T
                    link(dve.tensor_copy(to[:, 3 * n * T:3 * n * T + width], ps[:, 2 * a + n, 0:width]))
            dve.sem_inc(S["edge_kept"], 1)
            dve.wait_ge(S["range_spread"], 1)
            link(dve.tensor_scalar(rng[:, 0:1], lane[:, :], 1.0 * WD, None, ALU.mult))
            link(dve.tensor_scalar(rng[:, 1:2], lane[:, :], 1.0 * WD, WD - 1.0, ALU.mult, ALU.add))
            for n in range(2):
                width = min(3, CB - 3 * n) * T
                at = slice(3 * n * T, 3 * n * T + width)
                link(dve.tensor_scalar(hit[0:NW, 0, at], ps[0:NW, 2 + n, 0:width], rng[0:NW, 0:1], None, ALU.is_ge))
                link(dve.scalar_tensor_tensor(hit[0:NW, 1, at], ps[0:NW, n, 0:width], rng[0:NW, 1:2], hit[0:NW, 0, at],
                                              ALU.is_le, ALU.mult))
            link(dve.scalar_tensor_tensor(hit[0:NW, 2], iota[0:NW, 0:C], 1.0, hit[0:NW, 1], ALU.add, ALU.mult))
            link(dve.tensor_reduce(rng[0:NW, 2:3], hit[0:NW, 2], AX.X, ALU.max))
            link(dve.tensor_scalar(hit[0:NW, 0], iota[0:NW, 0:C], -1.0, 1.0 * C, ALU.mult, ALU.add))
            link(dve.tensor_tensor(hit[0:NW, 2], hit[0:NW, 0], hit[0:NW, 1], ALU.mult))
            link(dve.tensor_reduce(rng[0:NW, 3:4], hit[0:NW, 2], AX.X, ALU.max))
            link(dve.tensor_scalar(rng[0:NW, 4:5], rng[0:NW, 3:4], -0.5, C / 2 - 0.25, ALU.mult, ALU.add))
            link(dve.tensor_scalar(rng[0:NW, 4:5], rng[0:NW, 4:5], ROUND, ROUND, ALU.add, ALU.subtract))
            link(dve.tensor_scalar(rng[0:NW, 5:6], rng[0:NW, 2:3], 0.5, 0.25, ALU.mult, ALU.add))
            link(dve.tensor_scalar(rng[0:NW, 5:6], rng[0:NW, 5:6], ROUND, ROUND, ALU.add, ALU.subtract))
            link(dve.tensor_scalar(rng[0:NW, 6:7], rng[0:NW, 4:5], 1.0, None, ALU.add))
            link(dve.tensor_tensor(rng[0:NW, 5:6], rng[0:NW, 5:6], rng[0:NW, 6:7], ALU.max))
            link(dve.tensor_copy(rng_i[0:NW, :], rng[0:NW, 4:6]))
            dve.sem_inc(S["range_out"], 1)
            dve.wait_ge(S["weights_in"], 16 * H)
            dve.wait_ge(S["attn_in"], 32)
            for k in range(KF):
                for a in range(2):
                    link(dve.tensor_tensor(prod, wmat[:, k, :], acol[a], ALU.mult))
                    link(dve.tensor_reduce(wa[:, k, a * H:(a + 1) * H], prod.rearrange("p (h f) -> p h f", h=H), AX.X, ALU.add))
            link(dve.memset(z[:, :, :, FH:FA], 1.0))
            dve.sem_inc(S["vec_made"], 1)

            def feature_kept(turned, xT_made, product, kept, attention):
                with dve.Fori(0, NT // 2) as i:
                    for b in range(2):
                        t = 2 * i + b
                        dve.wait_ge(turned, t + 3)
                        dve.tensor_copy(xT[b][:, 0:KF // 2, :],
                                        ps[:, 0, 0:KF // 2 * T].rearrange("p (k n) -> p k n", k=KF // 2)).then_inc(xT_made, 1)
                        dve.wait_ge(product, t + 1)
                        base = 2 + 3 * b
                        if attention:
                            dve.tensor_copy(elr[0:T, bass.ds(t, 1), :].rearrange("p o e -> p (o e)"), ps[0:T, base + 2, 0:2 * H])
                            dve.tensor_copy(z[:, bass.ds(t, 1), 0:H // 2, 0:FH].rearrange("p o h f -> p (o h) f"),
                                            ps[0:T, base, :].rearrange("p (h f) -> p h f", h=H // 2)).then_inc(kept, 1)
                        else:
                            dve.tensor_copy(sup[:, bass.ds(t, 1), 0:HALF].rearrange("p o f -> p (o f)"),
                                            ps[0:T, base, :]).then_inc(kept, 1)

            feature_kept(S["turned"], S["xT_made"], S["product"], S["z_kept"], True)
            dve.wait_ge(S["z_kept"], NT)
            link(dve.tensor_copy(part_f[0:T, :, 0, :], elr[0:T, :, 0:H]))
            link(dve.tensor_scalar(part_f[0:T, :, 1, :], elr[0:T, :, 0:H], SLOPE, None, ALU.mult))
            for j in range(PARTS):
                part = elc[0:T, :, :, R + j * H:R + (j + 1) * H]
                link(dve.tensor_copy(part, part_f[0:T]))
                if j < PARTS - 1:
                    link(dve.tensor_tensor(part_f[0:T], part_f[0:T], part, ALU.subtract))
            dve.sem_inc(S["elc_made"], 1)
            dve.wait_ge(S["el_turned"], 1)
            for n in range(2 * NT // 8):
                link(dve.tensor_copy(lrow[0:2 * R, 4 * n:4 * n + 4].rearrange("p t v n -> p (t v) n"),
                                     bf_view(n)[0:2 * R, :].rearrange("p (a n) -> p a n", a=8)[:, :, 0:T]))
            dve.sem_inc(S["lrow_made"], 1)

            dve.sem_inc(S["c_kept"], 1)
            dve.sem_inc(S["res_free"], 1)
            dve.sem_inc(S["agg_kept"], 1)
            dve.sem_inc(S["prob_done"], 2)
            dve.sem_inc(S["emax_done"], 2)
            dve.wait_ge(S["range_in"], 32)
            base_chain = n_chain[0]
            step = dve.alloc_register("dve_step")
            dve.reg_mov(step, 0)
            TILE_LINKS = 32

            with dve.Fori(0, NT) as t:
                m = [0]

                def link_t(ins):
                    m[0] += 1
                    ins.then_inc(S["chain"], 1)
                    dve.wait_ge(S["chain"], TILE_LINKS * t + base_chain + m[0])

                bounds = []
                for w in range(WT):
                    bounds.append((dve.value_load(ranges[0:1, bass.ds(2 * WT * t + 2 * w, 1)], min_val=0, max_val=PAIRS - 1),
                                   dve.value_load(ranges[0:1, bass.ds(2 * WT * t + 2 * w + 1, 1)], min_val=1, max_val=PAIRS)))
                for w in range(WT):
                    with dve.Fori(*bounds[w]) as g:
                        n = dve.snap(step, min_val=0, max_val=NW * PAIRS)
                        for j in range(2):
                            dve.wait_ge(used[j], n + 1)
                            dve.tensor_scalar(onehot_s[j][:, :], iota[:, 0:T], low[:, bass.ds(2 * g + j, 1)], None, ALU.is_equal)
                            dve.tensor_scalar(onehot_d[j][:, :], iota[:, 0:WC], 1.0 * w * WC, key[:, bass.ds(2 * g + j, 1)],
                                              ALU.add, ALU.is_equal).then_inc(made[j], 1)
                        dve.reg_add(step, step, 1)
                    n = dve.snap(step, min_val=0, max_val=NW * PAIRS)
                    dve.wait_ge(used[1], n + 1)
                    dve.tensor_copy(count[:, :, w * WD:(w + 1) * WD].rearrange("p s d -> p d s"),
                                    ps[0:T, 4 + 2 * (w % 2), 0:WC].rearrange("p (d s) -> p d s", d=WD)).then_inc(S["c_kept"], 1)
                link_t(dve.tensor_scalar(key[:, 0:C], key[:, 0:C], -1.0 * T * NT, None, ALU.add))
                dve.wait_ge(S["c_kept"], WT * t + WT + 1)
                link_t(dve.tensor_scalar(absent, count, 0.0, -BIG, ALU.is_equal, ALU.mult))
                for h in range(H):
                    link_t(dve.tensor_tensor(reach, absent, elr[0:T, :, h:h + 1].to_broadcast([T, NT, T]), ALU.add))
                    link_t(dve.tensor_reduce(peak[0:T, h, :], reach.rearrange("p s d -> p d s"), AX.X, ALU.max))
                dve.sem_inc(S["peak_made"], 1)
                dve.wait_ge(S["peak_turned"], t + 1)
                link_t(dve.tensor_reduce(small[0:T, 0, :], ps[0:T, 4, 0:H * T].rearrange("p (h s) -> p h s", h=H), AX.X, ALU.max))
                er = elr[0:T, bass.ds(t, 1), H:2 * H].rearrange("p o h -> p (o h)")
                link_t(dve.tensor_scalar(small[0:T, 1, :], small[0:T, 0, :], -BIG / 2, None, ALU.is_gt))
                link_t(dve.tensor_tensor(small[0:T, 2, :], small[0:T, 0, :], small[0:T, 1, :], ALU.mult))
                link_t(dve.tensor_tensor(small[0:T, 3, :], small[0:T, 2, :], er, ALU.add))
                link_t(dve.scalar_tensor_tensor(small[0:T, 4, :], small[0:T, 3, :], SLOPE, small[0:T, 3, :], ALU.mult, ALU.max))
                link_t(dve.tensor_tensor(q[0:T, 0, :], er, small[0:T, 4, :], ALU.subtract))
                link_t(dve.scalar_tensor_tensor(q[0:T, 1, :], er, SLOPE, small[0:T, 4, :], ALU.mult, ALU.subtract))
                for j in range(PARTS):
                    part = qc[0:T, :, j * H:(j + 1) * H]
                    link_t(dve.tensor_copy(part, q[0:T]))
                    if j < PARTS - 1:
                        link_t(dve.tensor_tensor(q[0:T], q[0:T], part, ALU.subtract))
                dve.sem_inc(S["q_made"], 1)
                dve.wait_ge(S["q_turned"], t + 1)
                for v in range(2):
                    link_t(dve.tensor_tensor(qrow[0:2 * R, v], bf_view(5)[0:2 * R, v * 128:v * 128 + T].rearrange("p (o n) -> p o n", o=1).to_broadcast([2 * R, H, T]),
                                             block_mask[0:2 * R], ALU.mult))
                dve.sem_inc(S["qrow_made"], 1)
                def larger(s, b):
                    dve.wait_ge(S["exp_done"], NT * t + s + 2)
                    dve.tensor_tensor(e_max[b][0:T], e_pos[b][0:T], e_neg[b][0:T], ALU.max).then_inc(S["emax_done"], 1)

                def probs(s0, final):
                    for u in range(4):
                        s = s0 + u
                        if not (final and u == 3):
                            larger(s + 1, (u + 1) % 2)
                        dve.wait_ge(S["emax_done"], NT * t + s + 3)
                        dve.wait_ge(S["agg_done"], NT * t + s + 1)
                        dve.scalar_tensor_tensor(prob[u][0:T], e_max[u % 2][0:T].rearrange("p (h d) -> p h d", h=H), 1.0,
                                                 count[:, bass.ds(s, 1), :].to_broadcast([T, H, T]),
                                                 ALU.min, ALU.mult).then_inc(S["prob_done"], 1)

                larger(0, 0)
                with dve.Fori(0, NT // 4 - 1) as g:
                    probs(4 * g, False)
                probs(NT - 4, True)
                dve.wait_ge(S["agg_done"], NT * t + NT + 4)
                sums = ps[0:T, 0:H, FH:FA].rearrange("p h o -> p (h o)")
                link_t(dve.tensor_scalar(small[0:T, 5, :], sums, 0.0, None, ALU.is_equal))
                link_t(dve.tensor_tensor(small[0:T, 6, :], small[0:T, 5, :], sums, ALU.add))
                link_t(dve.reciprocal(small[0:T, 7, :], small[0:T, 6, :]))
                dve.wait_ge(S["res_in"], 16 * t + 16)
                for h in range(H):
                    last = dve.scalar_tensor_tensor(xsum[:, h * FH:(h + 1) * FH], ps[0:T, h, 0:FH], small[0:T, 7, h:h + 1],
                                                    xres[:, h * FH:(h + 1) * FH], ALU.mult, ALU.add)
                link_t(last)
                dve.sem_inc(S["agg_kept"], 1)
                for n in range(2):
                    link_t(dve.bn_stats(stats[0:T, n, :], xsum[:, n * HALF:(n + 1) * HALF]))
                dve.sem_inc(S["res_free"], 1)
                link_t(dve.bn_aggr(moments[0:T, :], stats[0:T].rearrange("p n s -> p (n s)")))
                dve.tensor_scalar(spread[0:T, 0:1], moments[0:T, 1:2], EPS, None, ALU.add).then_inc(S["var_made"], 1)
                dve.wait_ge(S["std_made"], t + 1)
                link_t(dve.reciprocal(spread[0:T, 2:3], spread[0:T, 1:2]))
                dve.wait_ge(S["x1_free"], t + 1)
                dve.tensor_scalar(xnew, xsum, moments[0:T, 0:1], spread[0:T, 2:3], ALU.subtract, ALU.mult).then_inc(S["x1_made"], 1)
            assert m[0] == TILE_LINKS, m[0]
            n_chain[0] = base_chain + NT * TILE_LINKS

            feature_kept(S["l1_turned"], S["l1_xT_made"], S["l1_product"], S["l1_kept"], False)
            dve.sem_inc(S["l1_agg_kept"], 2)
            base2 = n_chain[0]
            L1_LINKS = 5
            with dve.Fori(0, NT // 2) as i:
                for b, arrived in enumerate((S["w2_in0"], S["w2_in1"])):
                    t = 2 * i + b
                    m2 = [0]

                    def link_1(ins):
                        m2[0] += 1
                        ins.then_inc(S["chain"], 1)
                        dve.wait_ge(S["chain"], L1_LINKS * t + base2 + m2[0])

                    dve.wait_ge(S["l1_agg"], t + 1)
                    dve.wait_ge(arrived, 32 * i + 32)
                    res = xres if b == 0 else work[0:T, 3 * F:4 * F]
                    for n in range(2):
                        last = dve.tensor_tensor(xsum[:, n * HALF:(n + 1) * HALF], ps[0:T, 2 * b + n, :],
                                                 res[:, n * HALF:(n + 1) * HALF], ALU.add)
                    link_1(last)
                    for n in range(2):
                        link_1(dve.bn_stats(stats[0:T, n, :], xsum[:, n * HALF:(n + 1) * HALF]))
                    dve.sem_inc(S["l1_agg_kept"], 1)
                    link_1(dve.bn_aggr(moments[0:T, :], stats[0:T].rearrange("p n s -> p (n s)")))
                    dve.tensor_scalar(spread[0:T, 0:1], moments[0:T, 1:2], EPS, None, ALU.add).then_inc(S["l1_var"], 1)
                    dve.wait_ge(S["l1_std"], t + 1)
                    link_1(dve.reciprocal(spread[0:T, 2:3], spread[0:T, 1:2]))
                    dve.wait_ge(S["l1_free"], t + 1)
                    dve.tensor_scalar(xnew, xsum, moments[0:T, 0:1], spread[0:T, 2:3], ALU.subtract, ALU.mult).then_inc(S["l1_made"], 1)
                    dve.wait_ge(S["l1_made"], t + 1)
                    assert m2[0] == L1_LINKS


_INS = ["x", "src", "dst", "edge_weight", "L0_gnn_W", "L0_gnn_a_l", "L0_gnn_a_r", "L1_gnn_W"]


def kernel(**inputs):
    import numpy as np
    import concourse.bacc as bacc
    from concourse.bass_utils import run_bass_kernel_spmd

    nc = bacc.Bacc("TRN2", target_bir_lowering=False, num_devices=1)
    arrays, args = {}, []
    for name in _INS:
        a = np.ascontiguousarray(inputs[name])
        arrays[f"in_{name}"] = a
        args.append(nc.dram_tensor(f"in_{name}", a.shape, mybir.dt.from_np(a.dtype), kind="ExternalInput").ap())
    out = nc.dram_tensor("out", inputs["x"].shape, mybir.dt.float32, kind="ExternalOutput").ap()
    gat_gcn_resnorm(nc, *args, out)
    r = run_bass_kernel_spmd(nc, [arrays], core_ids=[0])
    return r.results[0]["out"]
```

```python
import concourse.bass as bass
from concourse import mybir
from contextlib import ExitStack


def gat_gcn_resnorm(nc, x, src, dst, edge_weight, W0, a_l, a_r, W1, out):
    f32, f32r = mybir.dt.float32, mybir.dt.float32r
    bf16, f16, i32 = mybir.dt.bfloat16, mybir.dt.float16, mybir.dt.int32
    ALU, ACT, AX = mybir.AluOpType, mybir.ActivationFunctionType, mybir.AxisListType

    N, F = x.shape
    H, _, FH = W0.shape
    E = src.shape[0]
    T = 125
    NT = N // T
    KF = F // 128
    HALF = F // 2
    FA = FH + 1
    C = E // 128
    CB = C // T
    EB = CB * 128
    WD = 25
    WC = WD * NT
    WT = T // WD
    NW = N // WD
    SUBS = (13, 12)
    NS = len(SUBS)
    SUB0 = [sum(SUBS[:k]) for k in range(NS)]
    NB = 2 * NS * WT
    RING = 8
    PARTS = 3
    R = PARTS * H
    BIG = 1.0e30
    ROUND = 12582912.0
    SLOPE = 0.2
    EPS = 1e-5
    STEPS_MAX = NW * NS * C
    SHARE = [(0, 3), (3, 6), (6, 9), (9, 12), (12, NT)]
    assert N == NT * T and E == C * 128 and C == CB * T and NW <= 128 and WC <= 512 and sum(SUBS) == WD

    w2_dram = nc.dram_tensor("w2_dram", (NT, T, NT * T), f32, kind="Internal").ap()
    xraw_dram = nc.dram_tensor("xraw_dram", (NT, T, F), f32, kind="Internal").ap()
    range_dram = nc.dram_tensor("range_dram", (NW, 2 * NS), i32, kind="Internal").ap()
    x_t = x.rearrange("(t p) f -> t p f", p=T)
    out_t = out.rearrange("(t p) f -> t p f", p=T)

    def tile_of(dram, t):
        return dram[bass.ds(t, 1)].rearrange("o p f -> (o p) f")

    ctx = ExitStack()
    with ctx:
        def sem(name):
            return ctx.enter_context(nc.semaphore(name))

        SIZE = {f32: 4, f32r: 4, i32: 4, bf16: 2, f16: 2}
        BASE = (nc.sbuf_base + 31) // 32 * 32
        LIMIT = nc.sbuf_top - BASE

        class Region:

            def __init__(self, at):
                self.at = at

            def __call__(self, name, shape, dt=f32):
                n = SIZE[dt]
                for d in shape[1:]:
                    n *= d
                self.at = (self.at + 31) // 32 * 32
                t = nc.alloc_sbuf_tensor_at(name, shape, dt, offset=BASE + self.at)
                self.at += n
                assert self.at <= LIMIT, (name, self.at)
                return t

        every = Region(0)
        ident = every("ident", [128, 128])
        ident_b = every("ident_b", [128, 128], bf16)
        moments = every("moments", [128, NT, 2])
        rstd = every("rstd", [128, NT])
        stats = every("stats", [128, 2, 6])
        moments1 = every("moments1", [128, 2])
        spread = every("spread", [128, 3])

        l0 = Region(every.at)
        key = l0("key", [128, C])
        low = l0("low", [128, C])
        weight = [l0(f"weight{j}", [128, C]) for j in range(PARTS)]
        ranges = l0("ranges", [1, NT * NB], i32)
        iota = l0("iota", [128, WC], f16)
        lane = l0("lane", [128, 1])
        rng = l0("rng", [128, 8])
        rng_i = l0("rng_i", [128, 2 * NS], i32)
        elr = l0("elr", [128, NT, 2 * H])
        part_f = l0("part_f", [128, NT, 2, H])
        elc = l0("elc", [128, NT, 2, 2 * R], bf16)
        lrow = l0("lrow", [128, NT, 2, T], bf16)
        block_mask = l0("block_mask", [128, H, T], bf16)
        z = l0("z", [T, NT, H, FA])
        after_z = l0.at
        prodp = Region(after_z)
        w_hi = prodp("w_hi", [128, KF, F], f32r)
        w_lo = prodp("w_lo", [128, KF, F], f32r)
        wa = prodp("wa", [128, KF, 2 * H])
        wa_hl = prodp("wa_hl", [128, KF, 2, 2 * H], f32r)
        xt = [prodp(f"xt{b}", [T, F]) for b in range(2)]
        xT_hi = [prodp(f"xT_hi{b}", [128, KF, T], f32r) for b in range(2)]
        xT_lo = [prodp(f"xT_lo{b}", [128, KF, T], f32r) for b in range(2)]
        prep = Region(after_z - 4 * NT * H * FA)
        raw_i = prep("raw_i", [T, 2, CB, 128], i32)
        whi_r = prep("parts_b", [T, CB, 128], bf16)
        edge = prep("edge", [T, 9, CB, 128])
        diag = prep("diag", [T, 2 * CB, T])
        hit = prep("hit", [128, 3, C])
        ones = prep("ones", [128, 128])
        iota_i = prep("iota_i", [128, EB], i32)
        iota_f = prep("iota_f", [128, EB])
        lane_i = prep("lane_i", [128, 1], i32)
        assert prep.at <= after_z
        raww = Region(after_z - 4 * NT * H * FA)
        w_raw = raww("w_raw", [128, KF, F])
        acol = [raww(f"acol{n}", [128, F]) for n in range(2)]
        prod = raww("prod", [128, F])
        assert raww.at <= after_z
        agg = Region(after_z)
        count = agg("count", [T, 2, NT, T])
        wsum = agg("wsum", [T, NT, T])
        absent = agg("absent", [T, NT, WD])
        reach = agg("reach", [T, H, NT, WD])
        peak = agg("peak", [T, H, T])
        small = agg("small", [128, 12, H])
        q = agg("q", [T, 2, H])
        qc = agg("qc", [T, 2, 2 * R], bf16)
        qrow = agg("qrow", [128, 2, H, T], bf16)
        e_pos = [agg(f"e_pos{j}", [T, H * T]) for j in range(2)]
        e_neg = [agg(f"e_neg{j}", [T, H * T]) for j in range(2)]
        e_max = [agg(f"e_max{j}", [T, H * T]) for j in range(2)]
        prob = [agg(f"prob{j}", [T, H, T]) for j in range(4)]
        onehot_d = agg("onehot_d", [128, RING, WC], bf16)
        onehot_s = agg("onehot_s", [128, RING, T], bf16)
        weighted = [agg(f"weighted{j}", [128, RING, T], bf16) for j in range(PARTS)]
        xres = agg("xres", [T, F])
        xsum = agg("xsum", [T, F])

        l1 = Region(every.at)
        sup_hi = l1("sup_hi", [T, NT, F], f32r)
        sup_lo = l1("sup_lo", [T, NT, F], f32r)
        after_sup = l1.at
        l1p = Region(after_sup)
        w1_hi = l1p("w1_hi", [128, KF, HALF], f32r)
        w1_lo = l1p("w1_lo", [128, KF, HALF], f32r)
        yt = [l1p(f"yt{b}", [T, F]) for b in range(2)]
        yT_hi = [l1p(f"yT_hi{b}", [128, KF, T], f32r) for b in range(2)]
        yT_lo = [l1p(f"yT_lo{b}", [128, KF, T], f32r) for b in range(2)]
        w1raw = Region(l1p.at - 4 * 4 * KF * T)
        w1_raw = w1raw("w1_raw", [128, KF // 2, HALF])
        l1a = Region(after_sup)
        w2_raw = [l1a(f"w2_raw{b}", [T, NT, T]) for b in range(2)]
        NG = 4
        GS = NT // NG
        w2_hi = [l1a(f"w2_hi{g}", [T, GS, T], f32r) for g in range(NG)]
        w2_lo = [l1a(f"w2_lo{g}", [T, GS, T], f32r) for g in range(NG)]
        yres = [l1a(f"yres{b}", [T, F]) for b in range(2)]
        ysum = l1a("ysum", [T, F])
        ynew = l1a("ynew", [T, F])

        ps = ctx.enter_context(nc.psum_tensor("ps", [128, 8, 512], f32))
        COUNT, WSUM, SCORE = 4, 5, 6

        def bf_view(bank):
            return ps[:, bank, :].bitcast(bf16)

        names = """edges_in weights_in attn_in const_made const_self range_out range_in
            edge_made edge_turned edge_kept diag_made range_spread vec_made waw
            x0_in x1_in turned xT_hi_made xT_lo_made product z_kept z_kept_act elc_made el_turned lrow_made
            made weighted_act weighted_pool used bank_kept absent_made reach_made peak_part wsum_free w2_out
            peak_made peak_turned top_made q_made q_turned qrow_made scores exp_done emax_done prob_done
            agg_done agg_kept res_in res_free xsum_made xsum_out xsum_free chain chain_pool
            rstd_var rstd_std w1_in w1_split
            y0_in y1_in y_norm y_turned yT_hi_made yT_lo_made y_product sup_hi_made sup_lo_made
            w2_in0 w2_in1 w2_hi_made w2_lo_made group_used l1_agg l1_agg_kept l1_var l1_std l1_made l1_out
            l1_free""".split()
        S = {n: sem(n) for n in names}

        block = ctx.enter_context(nc.Block())

        def load_bounds(eng, regs, tile):
            eng.load(regs, ranges[0:1, bass.ds(NB * tile, NB)])
            return [(eng.snap(regs[2 * k], min_val=0, max_val=C - 2), eng.snap(regs[2 * k + 1], min_val=2, max_val=C))
                    for k in range(NB // 2)]

        @block.sync
        def _(sp):
            sp.dma_start(raw_i[:, 0], src.rearrange("(b r k) -> r b k", b=CB, r=T)).then_inc(S["edges_in"], 16)
            sp.dma_start(raw_i[:, 1], dst.rearrange("(b r k) -> r b k", b=CB, r=T)).then_inc(S["edges_in"], 16)
            sp.dma_start(edge[:, 0], edge_weight.rearrange("(b r k) -> r b k", b=CB, r=T)).then_inc(S["edges_in"], 16)
            for b, arrived in enumerate((S["x0_in"], S["x1_in"])):
                sp.dma_start(xt[b][:, :], x_t[b]).then_inc(arrived, 16)
            sp.wait_ge(S["range_out"], 1)
            for h in range(H):
                sp.dma_start(w_raw[:, :, h * FH:(h + 1) * FH],
                             W0[h].rearrange("(k p) f -> p k f", p=128)).then_inc(S["weights_in"], 16)
            for n, a in enumerate((a_l, a_r)):
                sp.dma_start(acol[n][:, :], a.rearrange("(o h) f -> o (h f)", o=1).to_broadcast([128, F])).then_inc(S["attn_in"], 16)
            sp.dma_start(range_dram, rng_i[0:NW, :]).then_inc(S["range_in"], 16)
            sp.wait_ge(S["range_in"], 16)
            sp.dma_start(ranges[:, :], range_dram.rearrange("(o w) r -> o (w r)", o=1)).then_inc(S["range_in"], 16)
            with sp.Fori(1, NT // 2) as i:
                for b, arrived in enumerate((S["x0_in"], S["x1_in"])):
                    sp.wait_ge(S["turned"], 2 * i + b - 1)
                    sp.dma_start(xt[b][:, :], tile_of(x_t, 2 * i + b)).then_inc(arrived, 16)
            sp.wait_ge(S["z_kept"], NT)
            sp.wait_ge(S["z_kept_act"], NT)

            def weights_out(t):
                sp.wait_ge(S["bank_kept"], WT * t + WT + 1)
                sp.dma_start(tile_of(w2_dram, t), wsum.rearrange("p s d -> p (s d)")).then_inc(S["w2_out"], 16)
                sp.wait_ge(S["w2_out"], 16 * t + 16)
                sp.sem_inc(S["wsum_free"], 1)

            def rows_in_out(t):
                sp.wait_ge(S["xsum_made"], t + 1)
                sp.dma_start(tile_of(xraw_dram, t), xsum[:, :]).then_inc(S["xsum_out"], 16)
                sp.wait_ge(S["xsum_out"], 16 * t + 16)
                sp.sem_inc(S["xsum_free"], 1)

            def residual_in(t):
                sp.wait_ge(S["res_free"], t + 1)
                sp.dma_start(xres[:, :], tile_of(x_t, t)).then_inc(S["res_in"], 16)

            sp.sem_inc(S["wsum_free"], 1)
            sp.sem_inc(S["xsum_free"], 1)
            weights_out(0)
            with sp.Fori(0, NT - 1) as t:
                residual_in(t)
                weights_out(t + 1)
                rows_in_out(t)
            residual_in(NT - 1)
            rows_in_out(NT - 1)
            sp.wait_ge(S["rstd_var"], 1)
            for n in range(2):
                for m in range(2):
                    if 2 * n + m:
                        sp.wait_ge(S["w1_split"], 2 * n + m)
                    if n and not m:
                        sp.wait_ge(S["sup_lo_made"], NT)
                        sp.wait_ge(S["sup_hi_made"], NT)
                    sp.dma_start(w1_raw[:, :, :],
                                 W1.rearrange("(m k p) f -> m p k f", m=2, p=128)[m, :, :, n * HALF:(n + 1) * HALF]).then_inc(S["w1_in"], 16)
                with sp.Fori(0, NT // 2) as i:
                    for b, arrived in enumerate((S["y0_in"], S["y1_in"])):
                        sp.wait_ge(S["y_turned"], NT * n + 2 * i + b + 1)
                        sp.dma_start(yt[b][:, :], tile_of(xraw_dram, 2 * i + b)).then_inc(arrived, 16)
            sp.wait_ge(S["sup_lo_made"], 2 * NT)
            sp.wait_ge(S["sup_hi_made"], 2 * NT)
            arrived1 = (S["w2_in0"], S["w2_in1"])

            def tile_in(t, b):
                sp.dma_start(w2_raw[b].rearrange("p s d -> p (s d)"), tile_of(w2_dram, t)).then_inc(arrived1[b], 16)
                sp.dma_start(yres[b][:, :], tile_of(xraw_dram, t)).then_inc(arrived1[b], 16)

            def tile_out(t):
                sp.wait_ge(S["l1_made"], t + 1)
                sp.dma_start(tile_of(out_t, t), ynew[:, :]).then_inc(S["l1_out"], 16)
                sp.wait_ge(S["l1_out"], 16 * t + 16)
                sp.sem_inc(S["l1_free"], 1)

            sp.sem_inc(S["l1_free"], 1)
            for b in range(2):
                tile_in(b, b)
            with sp.Fori(0, NT // 2 - 1) as i:
                for b in range(2):
                    sp.wait_ge(S["l1_agg_kept"], 2 * i + b + 3)
                    tile_in(2 * i + b + 2, b)
                    tile_out(2 * i + b)
            for b in range(2):
                tile_out(NT - 2 + b)
            sp.wait_ge(S["l1_out"], 16 * NT)

        @block.gpsimd
        def _(pool):
            n = [0]

            def link(ins):
                n[0] += 1
                ins.then_inc(S["const_self"], 1)
                pool.wait_ge(S["const_self"], n[0])

            link(pool.iota(iota_i[:], pattern=[[1, EB]], base=0, channel_multiplier=0))
            link(pool.iota(lane_i[:], pattern=[[0, 1]], base=0, channel_multiplier=1))
            link(pool.tensor_copy(iota_f[:], iota_i[:]))
            link(pool.tensor_copy(iota[:], iota_i[:, 0:WC]))
            link(pool.tensor_copy(lane[:], lane_i[:]))
            link(pool.memset(ident[:], 0.0))
            link(pool.affine_select(out=ident[:], in_=ident[:], compare_op=ALU.not_equal, fill=1.0,
                                    base=0, pattern=[[-1, 128]], channel_multiplier=1))
            link(pool.tensor_copy(ident_b[:], ident[:]))
            link(pool.memset(ones[:], 1.0))
            link(pool.memset(block_mask[:], 0.0))
            for j in range(2 * PARTS):
                link(pool.affine_select(out=block_mask[:], in_=block_mask[:], compare_op=ALU.not_equal, fill=1.0,
                                        base=-j * H, pattern=[[-1, H], [0, T]], channel_multiplier=1))
            link(pool.memset(elc[:], 1.0))
            link(pool.memset(lrow[:], 0.0))
            pool.sem_inc(S["const_made"], 1)

            pool.wait_ge(S["z_kept"], NT)
            pool.wait_ge(S["z_kept_act"], NT)
            link(pool.memset(qc[:], 1.0))
            link(pool.memset(qrow[:], 0.0))
            pool.sem_inc(S["const_made"], 1)
            pool.wait_ge(S["lrow_made"], 1)
            pool.wait_ge(S["range_in"], 32)
            pool.sem_inc(S["reach_made"], 1)
            regs = [pool.alloc_register(f"pool_bound{k}") for k in range(NB)]
            step = pool.alloc_register("pool_step")
            pool.reg_mov(step, 0)
            links = pool.alloc_register("pool_links")
            pool.reg_mov(links, 0)
            tops = pool.alloc_register("pool_tops")
            pool.reg_mov(tops, 0)

            def windows(bounds, a, w):
                for k in range(NS):
                    with pool.Fori(*bounds[NS * w + k]) as c:
                        m = pool.snap(step, min_val=0, max_val=STEPS_MAX)
                        slot = pool.snap(m & (RING - 1), min_val=0, max_val=RING - 1)
                        pool.wait_ge(S["made"], m + 1)
                        pool.reg_add(step, step, 1)
                        pool.tensor_tensor(weighted[2][:, bass.ds(slot, 1), :].rearrange("p o s -> p (o s)"),
                                           onehot_s[:, bass.ds(slot, 1), :].rearrange("p o s -> p (o s)"),
                                           weight[2][:, bass.ds(c, 1)].to_broadcast([128, T]),
                                           ALU.mult).then_inc(S["weighted_pool"], 1)
                pool.wait_ge(S["absent_made"], WT * a + w + 2)
                pool.wait_ge(S["peak_part"], WT * a + w + 1)
                pool.tensor_tensor(reach[:, :, :, :], absent.rearrange("p (o s) d -> p o s d", o=1).to_broadcast([T, H, NT, WD]),
                                   elr[0:T, :, 0:H].rearrange("p s (h o) -> p h s o", o=1).to_broadcast([T, H, NT, WD]),
                                   ALU.add).then_inc(S["reach_made"], 1)

            def softmax_rows(a):
                m = [0]

                def link_a(ins):
                    m[0] += 1
                    ins.then_inc(S["chain_pool"], 1)
                    pool.wait_ge(S["chain_pool"], pool.snap(links, min_val=0, max_val=NT * POOL_LINKS) + 1)
                    pool.reg_add(links, links, 1)

                top, has, er = small[0:T, 0, :], small[0:T, 1, :], small[0:T, 11, :]
                link_a(pool.tensor_copy(er, elr[0:T, bass.ds(a, 1), H:2 * H].rearrange("p o h -> p (o h)")))
                pool.wait_ge(S["top_made"], pool.snap(tops, min_val=0, max_val=NT) + 1)
                pool.reg_add(tops, tops, 1)
                link_a(pool.tensor_scalar(has, top, -BIG / 2, None, ALU.is_gt))
                link_a(pool.tensor_tensor(small[0:T, 2, :], top, has, ALU.mult))
                link_a(pool.tensor_tensor(small[0:T, 3, :], small[0:T, 2, :], er, ALU.add))
                link_a(pool.tensor_scalar(small[0:T, 4, :], small[0:T, 3, :], 0.0, 1.0 - SLOPE, ALU.max, ALU.mult))
                link_a(pool.tensor_scalar(small[0:T, 8, :], small[0:T, 3, :], SLOPE, None, ALU.mult))
                link_a(pool.tensor_tensor(small[0:T, 9, :], small[0:T, 8, :], small[0:T, 4, :], ALU.add))
                link_a(pool.tensor_tensor(q[:, 0, :], er, small[0:T, 9, :], ALU.subtract))
                link_a(pool.tensor_scalar(small[0:T, 10, :], er, SLOPE, None, ALU.mult))
                link_a(pool.tensor_tensor(q[:, 1, :], small[0:T, 10, :], small[0:T, 9, :], ALU.subtract))
                for j in range(PARTS):
                    part = qc[:, :, j * H:(j + 1) * H]
                    link_a(pool.tensor_copy(part, q[:, :, :]))
                    if j < PARTS - 1:
                        link_a(pool.tensor_tensor(q[:, :, :], q[:, :, :], part, ALU.subtract))
                assert m[0] == POOL_LINKS, m[0]
                pool.sem_inc(S["q_made"], 1)

            POOL_LINKS = 15
            bounds = load_bounds(pool, regs, 0)
            for w in range(WT):
                windows(bounds, 0, w)
            softmax_rows(0)
            with pool.Fori(0, NT - 1) as t:
                bounds = load_bounds(pool, regs, t + 1)
                for w in range(WT):
                    windows(bounds, t + 1, w)
                softmax_rows(t + 1)

        def three_products(pe, to, left_hi, left_lo, right_hi, right_lo, first, last):
            pe.matmul(to, left_hi, right_hi, start=first, stop=False)
            pe.matmul(to, left_hi, right_lo, start=False, stop=False)
            return pe.matmul(to, left_lo, right_hi, start=False, stop=last)

        def turn(pe, tiles, arrived, done, t, b, turned):
            pe.wait_ge(arrived[b], done)
            for k in range(KF):
                last = pe.transpose(ps[:, k // 4, (k % 4) * T:(k % 4 + 1) * T],
                                    tiles[b][:, k * 128:(k + 1) * 128], ident[0:T, 0:T])
            last.then_inc(turned, 1)

        @block.tensor
        def _(pe):
            pe.wait_ge(S["const_made"], 1)
            pe.wait_ge(S["edge_made"], 1)
            for a in range(2 + PARTS):
                if a == 4:
                    pe.wait_ge(S["edge_kept"], 1)
                for b in range(CB):
                    last = pe.transpose(ps[:, 2 * (a % 4) + b // 3, (b % 3) * T:(b % 3 + 1) * T], edge[:, 1 + a, b, :], ident[0:T, 0:T])
                last.then_inc(S["edge_turned"], 1)
            pe.wait_ge(S["diag_made"], 1)
            for a in range(2):
                for b in range(CB):
                    last = pe.matmul(ps[0:T, 2 + 2 * a + b // 3, (b % 3) * T:(b % 3 + 1) * T], ones[0:T, 0:T],
                                     diag[:, a * CB + b, :], start=True, stop=True)
            last.then_inc(S["range_spread"], 1)

            xs = (S["x0_in"], S["x1_in"])
            pe.wait_ge(S["vec_made"], 1)
            turn(pe, xt, xs, 16, 0, 0, S["turned"])

            def features(i, final):
                for b in range(2):
                    t = 2 * i + b
                    pe.wait_ge(S["xT_lo_made"], t + 1)
                    if not (final and b):
                        turn(pe, xt, xs, 16 * i + 16 + 16 * b, t + 1, 1 - b, S["turned"])
                    base = 2 + 3 * b
                    for n in range(2):
                        at = slice(n * HALF, (n + 1) * HALF)
                        for k in range(KF):
                            three_products(pe, ps[0:T, base + n, :], xT_hi[b][:, k, :], xT_lo[b][:, k, :],
                                           w_hi[:, k, at], w_lo[:, k, at], k == 0, k == KF - 1)
                    for k in range(KF):
                        last = three_products(pe, ps[0:T, base + 2, 0:2 * H], xT_hi[b][:, k, :], xT_lo[b][:, k, :],
                                              wa_hl[:, k, 0, :], wa_hl[:, k, 1, :], k == 0, k == KF - 1)
                    last.then_inc(S["product"], 1)

            with pe.Fori(0, NT // 2 - 1) as i:
                features(i, False)
            features(NT // 2 - 1, True)

            pe.wait_ge(S["elc_made"], 1)
            pe.wait_ge(S["z_kept_act"], NT)
            for t in range(NT):
                for v in range(2):
                    n = 2 * t + v
                    last = pe.transpose(bf_view(n // 8)[0:2 * R, (n % 8) * 128:(n % 8) * 128 + T],
                                        elc[0:T, t, v, :], ident_b[0:T, 0:T])
            last.then_inc(S["el_turned"], 1)
            pe.wait_ge(S["lrow_made"], 1)
            pe.wait_ge(S["const_made"], 2)
            pe.wait_ge(S["range_in"], 32)

            pe.sem_inc(S["used"], RING)
            pe.sem_inc(S["agg_done"], 4)
            regs = [pe.alloc_register(f"pe_bound{k}") for k in range(NB)]
            step = pe.alloc_register("pe_step")
            pe.reg_mov(step, 0)

            def count_chunk(c, w, k, first):
                m = pe.snap(step, min_val=0, max_val=STEPS_MAX)
                slot = pe.snap(m & (RING - 1), min_val=0, max_val=RING - 1)
                at = slice(SUB0[k] * NT, (SUB0[k] + SUBS[k]) * NT)
                columns = onehot_d[:, bass.ds(slot, 1), 0:SUBS[k] * NT].rearrange("p o d -> p (o d)")
                pe.wait_ge(S["made"], m + 1)
                pe.matmul(ps[0:T, COUNT, at], onehot_s[:, bass.ds(slot, 1), :].rearrange("p o s -> p (o s)"), columns,
                          start=first, stop=True, skip_group_check=True)
                pe.wait_ge(S["weighted_act"], m + 1)
                pe.wait_ge(S["weighted_pool"], m + 1)
                for j in range(PARTS):
                    last = pe.matmul(ps[0:T, WSUM, at], weighted[j][:, bass.ds(slot, 1), :].rearrange("p o s -> p (o s)"), columns,
                                     start=first and j == 0, stop=True, skip_group_check=True)
                last.then_inc(S["used"], 1)
                pe.reg_add(step, step, 1)

            def windows(bounds, a, w):
                pe.wait_ge(S["bank_kept"], WT * a + w + 1)
                for k in range(NS):
                    first, end = bounds[NS * w + k]
                    count_chunk(first, w, k, True)
                    with pe.Fori(first + 1, end) as c:
                        count_chunk(c, w, k, False)

            def turn_peaks(a):
                pe.wait_ge(S["peak_made"], a + 1)
                pe.wait_ge(S["bank_kept"], WT * a + WT + 1)
                for h in range(H):
                    last = pe.transpose(ps[0:T, COUNT, h * T:(h + 1) * T], peak[:, h, :], ident[0:T, 0:T])
                last.then_inc(S["peak_turned"], 1)

            def turn_logits(a):
                pe.wait_ge(S["q_made"], a + 1)
                for v in range(2):
                    last = pe.transpose(bf_view(WSUM)[0:2 * R, v * 128:v * 128 + T], qc[:, v, :], ident_b[0:T, 0:T])
                last.then_inc(S["q_turned"], 1)

            def scores(t, s):
                pe.wait_ge(S["exp_done"], NT * t + s + 1)
                for v in range(2):
                    last = pe.matmul(ps[0:T, SCORE + v, 0:H * T], lrow[:, s, v, :],
                                     qrow[:, v].rearrange("p h d -> p (h d)"), start=True, stop=True)
                last.then_inc(S["scores"], 1)

            def attend(t, s):
                pe.wait_ge(S["prob_done"], NT * t + s + 3)
                for h in range(H):
                    last = pe.matmul(ps[0:T, h, 0:FA], prob[s % 4][:, h, :], z[:, s, h, :],
                                     start=(s == 0), stop=(s == NT - 1))
                last.then_inc(S["agg_done"], 1)

            def tile(t, bounds):
                pe.wait_ge(S["qrow_made"], t + 1)
                scores(t, 0)
                for w, (s0, s1) in enumerate(SHARE):
                    if bounds:
                        windows(bounds, t + 1, w)
                    if w == 0:
                        pe.wait_ge(S["agg_kept"], t + 1)
                    for s in range(s0, s1):
                        if s + 1 < NT:
                            scores(t, s + 1)
                        if bounds and s == NT - 4:
                            turn_peaks(t + 1)
                        if bounds and s == NT - 1:
                            turn_logits(t + 1)
                        attend(t, s)

            bounds = load_bounds(pe, regs, 0)
            for w in range(WT):
                windows(bounds, 0, w)
            turn_peaks(0)
            turn_logits(0)
            with pe.Fori(0, NT - 1) as t:
                bounds = load_bounds(pe, regs, t + 1)
                tile(t, bounds)
            tile(NT - 1, None)

            pe.wait_ge(S["agg_kept"], NT + 1)
            ys = (S["y0_in"], S["y1_in"])
            pe.sem_inc(S["y_turned"], 2)
            for n in range(2):
                pe.wait_ge(S["w1_split"], 2 * n + 2)
                pe.wait_ge(S["y_norm"], NT * n + 1)
                turn(pe, yt, ys, 16 * (NT // 2) * n + 16, 0, 0, S["y_turned"])

                def features1(i, final):
                    for b in range(2):
                        t = 2 * i + b
                        pe.wait_ge(S["yT_lo_made"], NT * n + t + 1)
                        if not (final and b):
                            pe.wait_ge(S["y_norm"], NT * n + t + 2)
                            turn(pe, yt, ys, 16 * (NT // 2) * n + 16 * i + 16 + 16 * b, t + 1, 1 - b, S["y_turned"])
                        for k in range(KF):
                            last = three_products(pe, ps[0:T, 2 + b, :], yT_hi[b][:, k, :], yT_lo[b][:, k, :],
                                                  w1_hi[:, k, :], w1_lo[:, k, :], k == 0, k == KF - 1)
                        last.then_inc(S["y_product"], 1)

                with pe.Fori(0, NT // 2 - 1) as i:
                    features1(i, False)
                features1(NT // 2 - 1, True)

            pe.wait_ge(S["sup_lo_made"], 2 * NT)
            pe.sem_inc(S["group_used"], NG)
            with pe.Fori(0, NT // 2) as i:
                for b in range(2):
                    t = 2 * i + b
                    pe.wait_ge(S["l1_agg_kept"], t + 1)
                    for g in range(NG):
                        pe.wait_ge(S["w2_lo_made"], NG * t + g + 1)
                        for s in range(GS):
                            for n in range(2):
                                at = slice(n * HALF, (n + 1) * HALF)
                                last = three_products(pe, ps[0:T, 2 * b + n, :], w2_hi[g][:, s, :], w2_lo[g][:, s, :],
                                                      sup_hi[:, GS * g + s, at], sup_lo[:, GS * g + s, at],
                                                      g == 0 and s == 0, g == NG - 1 and s == GS - 1)
                        last.then_inc(S["group_used"], 1)

        @block.scalar
        def _(act):
            def turned_hi(turned, t, xT, made):
                act.wait_ge(turned, t)
                act.activation(xT.rearrange("p (a k) n -> p a (k n)", a=2), ps[:, 0:2, 0:KF // 2 * T], ACT.Copy).then_inc(made, 1)

            turned_hi(S["turned"], 1, xT_hi[0], S["xT_hi_made"])

            def features(i, final):
                for b in range(2):
                    t = 2 * i + b
                    if not (final and b):
                        turned_hi(S["turned"], t + 2, xT_hi[1 - b], S["xT_hi_made"])
                    act.wait_ge(S["product"], t + 1)
                    act.activation(z[:, bass.ds(t, 1), H // 2:, 0:FH].rearrange("p o h f -> p (o h) f"),
                                   ps[0:T, 3 + 3 * b, :].rearrange("p (h f) -> p h f", h=H // 2), ACT.Copy).then_inc(S["z_kept_act"], 1)

            with act.Fori(0, NT // 2 - 1) as i:
                features(i, False)
            features(NT // 2 - 1, True)

            act.wait_ge(S["z_kept"], NT)
            act.wait_ge(S["range_in"], 32)
            act.sem_inc(S["bank_kept"], 1)
            act.sem_inc(S["exp_done"], 1)
            regs = [act.alloc_register(f"act_bound{k}") for k in range(NB)]
            step = act.alloc_register("act_step")
            act.reg_mov(step, 0)

            def windows(bounds, a, w):
                for k in range(NS):
                    with act.Fori(*bounds[NS * w + k]) as c:
                        m = act.snap(step, min_val=0, max_val=STEPS_MAX)
                        slot = act.snap(m & (RING - 1), min_val=0, max_val=RING - 1)
                        act.wait_ge(S["made"], m + 1)
                        for j in range(2):
                            last = act.activation(weighted[j][:, bass.ds(slot, 1), :].rearrange("p o s -> p (o s)"),
                                                  onehot_s[:, bass.ds(slot, 1), :].rearrange("p o s -> p (o s)"), ACT.Copy,
                                                  scale=weight[j][:, bass.ds(c, 1)])
                        last.then_inc(S["weighted_act"], 1)
                        act.reg_add(step, step, 1)

            def keep_banks(a, par, w):
                if w == 0:
                    act.wait_ge(S["wsum_free"], a + 1)
                m = act.snap(step, min_val=0, max_val=STEPS_MAX)
                act.wait_ge(S["used"], m + RING)
                at = slice(w * WD, (w + 1) * WD)
                act.activation(count[:, bass.ds(par, 1), :, at].rearrange("p o s d -> p d (o s)"),
                               ps[0:T, COUNT, 0:WC].rearrange("p (d s) -> p d s", d=WD), ACT.Copy)
                act.activation(wsum[:, :, at].rearrange("p s d -> p d s"),
                               ps[0:T, WSUM, 0:WC].rearrange("p (d s) -> p d s", d=WD), ACT.Copy).then_inc(S["bank_kept"], 1)

            def exps(t, s):
                act.wait_ge(S["scores"], NT * t + s + 1)
                act.wait_ge(S["emax_done"], NT * t + s + 1)
                act.activation(e_pos[s % 2][:, :], ps[0:T, SCORE, 0:H * T], ACT.Exp)
                act.activation(e_neg[s % 2][:, :], ps[0:T, SCORE + 1, 0:H * T], ACT.Exp).then_inc(S["exp_done"], 1)

            def tile(t, bounds):
                for w, (s0, s1) in enumerate(SHARE):
                    exps(t, s0)
                    if bounds:
                        windows(bounds, t + 1, w)
                    exps(t, s0 + 1)
                    if bounds:
                        keep_banks(t + 1, (t + 1) & 1, w)
                    for s in range(s0 + 2, s1):
                        exps(t, s)

            bounds = load_bounds(act, regs, 0)
            for w in range(WT):
                windows(bounds, 0, w)
                keep_banks(0, 0, w)
            with act.Fori(0, NT - 1) as t:
                bounds = load_bounds(act, regs, t + 1)
                tile(t, bounds)
            tile(NT - 1, None)

            act.wait_ge(S["rstd_var"], 1)
            act.activation(rstd[0:T, :], rstd[0:T, :], ACT.Sqrt).then_inc(S["rstd_std"], 1)
            for n in range(2):
                turned_hi(S["y_turned"], NT * n + 3, yT_hi[0], S["yT_hi_made"])

                def features1(i, final):
                    for b in range(2):
                        t = 2 * i + b
                        if not (final and b):
                            turned_hi(S["y_turned"], NT * n + t + 4, yT_hi[1 - b], S["yT_hi_made"])
                        act.wait_ge(S["y_product"], NT * n + t + 1)
                        act.activation(sup_hi[:, bass.ds(t, 1), n * HALF:(n + 1) * HALF].rearrange("p o f -> p (o f)"),
                                       ps[0:T, 2 + b, :], ACT.Copy).then_inc(S["sup_hi_made"], 1)

                with act.Fori(0, NT // 2 - 1) as i:
                    features1(i, False)
                features1(NT // 2 - 1, True)
            act.wait_ge(S["sup_lo_made"], 2 * NT)
            arrived1 = (S["w2_in0"], S["w2_in1"])

            def split_hi(t, b, arrivals):
                act.wait_ge(arrived1[b], 32 * arrivals)
                for g in range(NG):
                    act.wait_ge(S["group_used"], NG * t + g + 1)
                    act.activation(w2_hi[g][:, :, :], w2_raw[b][:, GS * g:GS * g + GS, :], ACT.Copy).then_inc(S["w2_hi_made"], 1)

            def pair(i, final):
                for b in range(2):
                    t = 2 * i + b
                    if not (final and b):
                        split_hi(t + 1, 1 - b, i + 1 + b)
                    act.wait_ge(S["l1_var"], t + 1)
                    act.activation(spread[0:T, 1:2], spread[0:T, 0:1], ACT.Sqrt).then_inc(S["l1_std"], 1)

            split_hi(0, 0, 1)
            with act.Fori(0, NT // 2 - 1) as i:
                pair(i, False)
            pair(NT // 2 - 1, True)

        @block.vector
        def _(dve):
            n_chain = [0]

            def link(ins):
                n_chain[0] += 1
                ins.then_inc(S["chain"], 1)
                dve.wait_ge(S["chain"], n_chain[0])

            def linker(per, index):
                base, m = n_chain[0], [0]

                def link_in(ins):
                    m[0] += 1
                    ins.then_inc(S["chain"], 1)
                    dve.wait_ge(S["chain"], index * per + base + m[0])
                return link_in, m

            dve.wait_ge(S["edges_in"], 48)
            srcf, dstf, hi_s = edge[:, 6], edge[:, 7], edge[:, 8]
            e_low, e_key, w_in = edge[:, 1], edge[:, 2], edge[:, 0]
            link(dve.tensor_copy(srcf, raw_i[:, 0]))
            link(dve.tensor_copy(dstf, raw_i[:, 1]))
            link(dve.tensor_scalar(hi_s, srcf, -(T // 2) * 1.0, 1.0 / T, ALU.add, ALU.mult))
            link(dve.tensor_scalar(hi_s, hi_s, ROUND, ROUND, ALU.add, ALU.subtract))
            link(dve.scalar_tensor_tensor(e_low, hi_s, -1.0 * T, srcf, ALU.mult, ALU.add))
            link(dve.scalar_tensor_tensor(e_key, dstf, 1.0 * NT, hi_s, ALU.mult, ALU.add))
            for j in range(PARTS):
                link(dve.tensor_copy(whi_r[:, :, :], w_in))
                link(dve.tensor_copy(edge[:, 3 + j], whi_r[:, :, :]))
                if j < PARTS - 1:
                    link(dve.tensor_tensor(w_in, w_in, edge[:, 3 + j], ALU.subtract))
            dve.sem_inc(S["edge_made"], 1)
            dve.wait_ge(S["const_made"], 1)
            link(dve.tensor_reduce(hit[0:T, 0, 0:CB], dstf, AX.X, ALU.min))
            link(dve.tensor_reduce(hit[0:T, 1, 0:CB], dstf, AX.X, ALU.max))
            for a in range(2):
                for b in range(CB):
                    link(dve.tensor_scalar(diag[:, a * CB + b, :], ident[0:T, 0:T], hit[0:T, a, b:b + 1], None, ALU.mult))
            for a, to in enumerate((low, key, *weight)):
                dve.wait_ge(S["edge_turned"], a + 1)
                for n in range(2):
                    width = min(3, CB - 3 * n) * T
                    link(dve.tensor_copy(to[:, 3 * n * T:3 * n * T + width], ps[:, 2 * (a % 4) + n, 0:width]))
                if a == 3:
                    dve.sem_inc(S["edge_kept"], 1)
                    dve.sem_inc(S["diag_made"], 1)
            dve.wait_ge(S["range_spread"], 1)
            for k in range(NS):
                lo, hi = rng[0:NW, 0:1], rng[0:NW, 1:2]
                link(dve.tensor_scalar(lo, lane[0:NW, :], 1.0 * WD, 1.0 * SUB0[k], ALU.mult, ALU.add))
                link(dve.tensor_scalar(hi, lane[0:NW, :], 1.0 * WD, SUB0[k] + SUBS[k] - 1.0, ALU.mult, ALU.add))
                for n in range(2):
                    width = min(3, CB - 3 * n) * T
                    at = slice(3 * n * T, 3 * n * T + width)
                    link(dve.tensor_scalar(hit[0:NW, 0, at], ps[0:NW, 4 + n, 0:width], lo, None, ALU.is_ge))
                    link(dve.scalar_tensor_tensor(hit[0:NW, 1, at], ps[0:NW, 2 + n, 0:width], hi, hit[0:NW, 0, at],
                                                  ALU.is_le, ALU.mult))
                link(dve.scalar_tensor_tensor(hit[0:NW, 2], iota_f[0:NW, 0:C], 1.0, hit[0:NW, 1], ALU.add, ALU.mult))
                link(dve.tensor_reduce(rng[0:NW, 2:3], hit[0:NW, 2], AX.X, ALU.max))
                link(dve.tensor_scalar(hit[0:NW, 0], iota_f[0:NW, 0:C], -1.0, 1.0 * C, ALU.mult, ALU.add))
                link(dve.tensor_tensor(hit[0:NW, 2], hit[0:NW, 0], hit[0:NW, 1], ALU.mult))
                link(dve.tensor_reduce(rng[0:NW, 3:4], hit[0:NW, 2], AX.X, ALU.max))
                link(dve.tensor_scalar(rng[0:NW, 4:5], rng[0:NW, 3:4], -1.0, 1.0 * C, ALU.mult, ALU.add))
                link(dve.tensor_scalar(rng[0:NW, 5:6], rng[0:NW, 4:5], C - 2.0, None, ALU.min))
                link(dve.tensor_scalar(rng[0:NW, 6:7], rng[0:NW, 5:6], 2.0, None, ALU.add))
                link(dve.tensor_tensor(rng[0:NW, 6:7], rng[0:NW, 6:7], rng[0:NW, 2:3], ALU.max))
                link(dve.tensor_copy(rng_i[0:NW, 2 * k:2 * k + 2], rng[0:NW, 5:7]))
            dve.sem_inc(S["range_out"], 1)
            dve.wait_ge(S["weights_in"], 16 * H)
            dve.wait_ge(S["attn_in"], 32)
            for k in range(KF):
                for a in range(2):
                    link(dve.tensor_tensor(prod[:, :], w_raw[:, k, :], acol[a][:, :], ALU.mult))
                    link(dve.tensor_reduce(wa[:, k, a * H:(a + 1) * H], prod.rearrange("p (h f) -> p h f", h=H), AX.X, ALU.add))
            link(dve.tensor_copy(wa_hl[:, :, 0, :], wa[:, :, :]))
            link(dve.tensor_tensor(wa_hl[:, :, 1, :], wa[:, :, :], wa_hl[:, :, 0, :].bitcast(f32), ALU.subtract))
            link(dve.tensor_copy(w_hi[:, :, :], w_raw[:, :, :]))
            link(dve.tensor_tensor(w_lo[:, :, :], w_raw[:, :, :], w_hi[:, :, :].bitcast(f32), ALU.subtract))
            link(dve.memset(z[:, :, :, FH:FA], 1.0))
            dve.sem_inc(S["vec_made"], 1)

            def turned_lo(hi_made, value, xT_h, xT_l, made):
                dve.wait_ge(hi_made, value)
                dve.tensor_tensor(xT_l.rearrange("p (a k) n -> p a (k n)", a=2), ps[:, 0:2, 0:KF // 2 * T],
                                  xT_h.rearrange("p (a k) n -> p a (k n)", a=2).bitcast(f32), ALU.subtract).then_inc(made, 1)

            turned_lo(S["xT_hi_made"], 1, xT_hi[0], xT_lo[0], S["xT_lo_made"])

            def features(i, final):
                for b in range(2):
                    t = 2 * i + b
                    if not (final and b):
                        turned_lo(S["xT_hi_made"], t + 2, xT_hi[1 - b], xT_lo[1 - b], S["xT_lo_made"])
                    dve.wait_ge(S["product"], t + 1)
                    dve.tensor_copy(elr[0:T, bass.ds(t, 1), :].rearrange("p o e -> p (o e)"), ps[0:T, 4 + 3 * b, 0:2 * H])
                    dve.tensor_copy(z[:, bass.ds(t, 1), 0:H // 2, 0:FH].rearrange("p o h f -> p (o h) f"),
                                    ps[0:T, 2 + 3 * b, :].rearrange("p (h f) -> p h f", h=H // 2)).then_inc(S["z_kept"], 1)

            with dve.Fori(0, NT // 2 - 1) as i:
                features(i, False)
            features(NT // 2 - 1, True)
            dve.wait_ge(S["z_kept"], NT)
            link(dve.tensor_copy(part_f[0:T, :, 0, :], elr[0:T, :, 0:H]))
            link(dve.tensor_scalar(part_f[0:T, :, 1, :], elr[0:T, :, 0:H], SLOPE, None, ALU.mult))
            for j in range(PARTS):
                part = elc[0:T, :, :, R + j * H:R + (j + 1) * H]
                link(dve.tensor_copy(part, part_f[0:T]))
                if j < PARTS - 1:
                    link(dve.tensor_tensor(part_f[0:T], part_f[0:T], part, ALU.subtract))
            dve.sem_inc(S["elc_made"], 1)
            dve.wait_ge(S["el_turned"], 1)
            for n in range(2 * NT // 8):
                link(dve.tensor_copy(lrow[0:2 * R, 4 * n:4 * n + 4].rearrange("p t v n -> p (t v) n"),
                                     bf_view(n)[0:2 * R, :].rearrange("p (a n) -> p a n", a=8)[:, :, 0:T]))
            dve.sem_inc(S["lrow_made"], 1)

            dve.wait_ge(S["z_kept_act"], NT)
            dve.wait_ge(S["const_made"], 2)
            dve.wait_ge(S["range_in"], 32)
            dve.sem_inc(S["absent_made"], 1)
            dve.sem_inc(S["peak_part"], 1)
            dve.sem_inc(S["res_free"], 1)
            dve.sem_inc(S["agg_kept"], 1)
            dve.sem_inc(S["prob_done"], 2)
            dve.sem_inc(S["emax_done"], 2)
            regs = [dve.alloc_register(f"dve_bound{k}") for k in range(NB)]
            step = dve.alloc_register("dve_step")
            dve.reg_mov(step, 0)

            def windows(bounds, w):
                for k in range(NS):
                    with dve.Fori(*bounds[NS * w + k]) as c:
                        m = dve.snap(step, min_val=0, max_val=STEPS_MAX)
                        slot = dve.snap(m & (RING - 1), min_val=0, max_val=RING - 1)
                        dve.wait_ge(S["used"], m + 1)
                        dve.tensor_scalar(onehot_s[:, bass.ds(slot, 1), :].rearrange("p o s -> p (o s)"), iota[:, 0:T],
                                          low[:, bass.ds(c, 1)], None, ALU.is_equal)
                        dve.tensor_scalar(onehot_d[:, bass.ds(slot, 1), 0:SUBS[k] * NT].rearrange("p o d -> p (o d)"),
                                          iota[:, 0:SUBS[k] * NT], 1.0 * (w * WD + SUB0[k]) * NT, key[:, bass.ds(c, 1)],
                                          ALU.add, ALU.is_equal).then_inc(S["made"], 1)
                        dve.reg_add(step, step, 1)

            def no_edge(a, par, w):
                dve.wait_ge(S["bank_kept"], WT * a + w + 2)
                dve.wait_ge(S["reach_made"], WT * a + w + 1)
                dve.tensor_scalar(absent[:, :, :], count[:, bass.ds(par, 1), :, w * WD:(w + 1) * WD].rearrange("p o s d -> p (o s) d"), 0.0, -BIG,
                                  ALU.is_equal, ALU.mult).then_inc(S["absent_made"], 1)

            def peaks(a, w):
                dve.wait_ge(S["reach_made"], WT * a + w + 2)
                dve.tensor_reduce(peak[:, :, w * WD:(w + 1) * WD], reach.rearrange("p h s d -> p h d s"), AX.X,
                                  ALU.max).then_inc(S["peak_part"], 1)
                if w == WT - 1:
                    dve.wait_ge(S["peak_part"], WT * a + WT + 1)
                    dve.sem_inc(S["peak_made"], 1)

            def top(a):
                dve.wait_ge(S["peak_turned"], a + 1)
                dve.tensor_reduce(small[0:T, 0, :], ps[0:T, COUNT, 0:H * T].rearrange("p (h s) -> p h s", h=H), AX.X,
                                  ALU.max).then_inc(S["top_made"], 1)

            def logits(a):
                dve.wait_ge(S["q_turned"], a + 1)
                for v in range(2):
                    last = dve.tensor_tensor(qrow[0:2 * R, v],
                                             bf_view(WSUM)[0:2 * R, v * 128:v * 128 + T].rearrange("p (o n) -> p o n", o=1).to_broadcast([2 * R, H, T]),
                                             block_mask[0:2 * R], ALU.mult)
                last.then_inc(S["qrow_made"], 1)

            def larger(t, s):
                dve.wait_ge(S["exp_done"], NT * t + s + 2)
                dve.tensor_tensor(e_max[s % 2][:, :], e_pos[s % 2][:, :], e_neg[s % 2][:, :], ALU.max).then_inc(S["emax_done"], 1)

            def probs(t, par, s):
                larger(t, s)
                dve.wait_ge(S["emax_done"], NT * t + s + 3)
                dve.wait_ge(S["agg_done"], NT * t + s + 1)
                dve.scalar_tensor_tensor(prob[s % 4][:, :, :], e_max[s % 2].rearrange("p (h d) -> p h d", h=H), 1.0,
                                         count[:, bass.ds(par, 1), s, :].to_broadcast([T, H, T]),
                                         ALU.min, ALU.mult).then_inc(S["prob_done"], 1)

            def rows(t, link_t):
                sums = ps[0:T, 0:H, FH:FA].rearrange("p h o -> p (h o)")
                dve.wait_ge(S["agg_done"], NT * t + NT + 4)
                link_t(dve.tensor_scalar(small[0:T, 5, :], sums, 0.0, None, ALU.is_equal))
                link_t(dve.tensor_tensor(small[0:T, 6, :], small[0:T, 5, :], sums, ALU.add))
                link_t(dve.reciprocal(small[0:T, 7, :], small[0:T, 6, :]))
                dve.wait_ge(S["res_in"], 16 * t + 16)
                dve.wait_ge(S["xsum_free"], t + 1)
                for h in range(H):
                    last = dve.scalar_tensor_tensor(xsum[:, h * FH:(h + 1) * FH], ps[0:T, h, 0:FH], small[0:T, 7, h:h + 1],
                                                    xres[:, h * FH:(h + 1) * FH], ALU.mult, ALU.add)
                link_t(last)
                dve.sem_inc(S["agg_kept"], 1)
                dve.sem_inc(S["xsum_made"], 1)
                for n in range(2):
                    link_t(dve.bn_stats(stats[0:T, n, :], xsum[:, n * HALF:(n + 1) * HALF]))
                dve.sem_inc(S["res_free"], 1)
                link_t(dve.bn_aggr(moments1[0:T, :], stats[0:T].rearrange("p n s -> p (n s)")))
                link_t(dve.tensor_copy(moments[0:T, bass.ds(t, 1), :].rearrange("p o m -> p (o m)"), moments1[0:T, :]))

            def tile(t, bounds, link_t):
                par = t & 1
                for w, (s0, s1) in enumerate(SHARE):
                    if bounds:
                        windows(bounds, w)
                    probs(t, par, s0)
                    if bounds and w:
                        peaks(t + 1, w - 1)
                    for s in range(s0 + 1, s1):
                        probs(t, par, s)
                        if bounds:
                            if s == s0 + 1:
                                no_edge(t + 1, (t + 1) & 1, w)
                            if w == WT - 1 and s == s0 + 3:
                                link_t(dve.tensor_scalar(key[:, :], key[:, :], -1.0 * T * NT, None, ALU.add))
                                peaks(t + 1, w)
                            if s == NT - 4:
                                top(t + 1)
                if bounds:
                    logits(t + 1)
                rows(t, link_t)

            bounds = load_bounds(dve, regs, 0)
            for w in range(WT):
                windows(bounds, w)
                no_edge(0, 0, w)
                peaks(0, w)
            link(dve.tensor_scalar(key[:, :], key[:, :], -1.0 * T * NT, None, ALU.add))
            top(0)
            logits(0)
            LINKS = 9
            with dve.Fori(0, NT - 1) as t:
                bounds = load_bounds(dve, regs, t + 1)
                link_t, m = linker(LINKS, t)
                tile(t, bounds, link_t)
            assert m[0] == LINKS, m[0]
            n_chain[0] += LINKS * (NT - 1)
            tile(NT - 1, None, link)

            link(dve.tensor_scalar(rstd[0:T, :], moments[0:T, :, 1], EPS, None, ALU.add))
            dve.sem_inc(S["rstd_var"], 1)
            dve.wait_ge(S["rstd_std"], 1)
            link(dve.reciprocal(rstd[0:T, :], rstd[0:T, :]))
            dve.wait_ge(S["xsum_free"], NT + 1)

            def normed(t):
                return moments[0:T, bass.ds(t, 1), 0:1].rearrange("p o m -> p (o m)"), rstd[0:T, bass.ds(t, 1)]

            ys = (S["y0_in"], S["y1_in"])
            for n in range(2):
                for m in range(2):
                    dve.wait_ge(S["w1_in"], 16 * (2 * n + m) + 16)
                    at = slice(m * KF // 2, (m + 1) * KF // 2)
                    link(dve.tensor_copy(w1_hi[:, at, :], w1_raw[:, :, :]))
                    link(dve.tensor_tensor(w1_lo[:, at, :], w1_raw[:, :, :], w1_hi[:, at, :].bitcast(f32), ALU.subtract))
                    dve.sem_inc(S["w1_split"], 1)

                def norm(t, b, count_in):
                    dve.wait_ge(ys[b], count_in)
                    mean, r = normed(t)
                    dve.tensor_scalar(yt[b][:, :], yt[b][:, :], mean, r, ALU.subtract, ALU.mult).then_inc(S["y_norm"], 1)

                first_in = 16 * (NT // 2) * n + 16
                norm(0, 0, first_in)
                turned_lo(S["yT_hi_made"], NT * n + 1, yT_hi[0], yT_lo[0], S["yT_lo_made"])

                def features1(i, final):
                    for b in range(2):
                        t = 2 * i + b
                        if not (final and b):
                            norm(t + 1, 1 - b, first_in + 16 * i + 16 * b)
                            turned_lo(S["yT_hi_made"], NT * n + t + 2, yT_hi[1 - b], yT_lo[1 - b], S["yT_lo_made"])
                        dve.wait_ge(S["sup_hi_made"], NT * n + t + 1)
                        at = slice(n * HALF, (n + 1) * HALF)
                        dve.tensor_tensor(sup_lo[:, bass.ds(t, 1), at].rearrange("p o f -> p (o f)"), ps[0:T, 2 + b, :],
                                          sup_hi[:, bass.ds(t, 1), at].rearrange("p o f -> p (o f)").bitcast(f32),
                                          ALU.subtract).then_inc(S["sup_lo_made"], 1)

                with dve.Fori(0, NT // 2 - 1) as i:
                    features1(i, False)
                features1(NT // 2 - 1, True)

            dve.sem_inc(S["l1_agg_kept"], 2)
            dve.wait_ge(S["sup_lo_made"], 2 * NT)

            arrived1 = (S["w2_in0"], S["w2_in1"])

            def split_lo(t, b, arrivals):
                dve.wait_ge(arrived1[b], 32 * arrivals)
                for g in range(NG):
                    dve.wait_ge(S["w2_hi_made"], NG * t + g + 1)
                    dve.tensor_tensor(w2_lo[g][:, :, :], w2_raw[b][:, GS * g:GS * g + GS, :], w2_hi[g][:, :, :].bitcast(f32),
                                      ALU.subtract).then_inc(S["w2_lo_made"], 1)

            def rows1(t, b, link_1):
                mean, r = normed(t)
                link_1(dve.tensor_scalar(yres[b][:, :], yres[b][:, :], mean, r, ALU.subtract, ALU.mult))
                dve.wait_ge(S["group_used"], NG * t + 2 * NG)
                for n in range(2):
                    last = dve.tensor_tensor(ysum[:, n * HALF:(n + 1) * HALF], ps[0:T, 2 * b + n, :],
                                             yres[b][:, n * HALF:(n + 1) * HALF], ALU.add)
                link_1(last)
                for n in range(2):
                    link_1(dve.bn_stats(stats[0:T, n, :], ysum[:, n * HALF:(n + 1) * HALF]))
                dve.sem_inc(S["l1_agg_kept"], 1)
                link_1(dve.bn_aggr(moments1[0:T, :], stats[0:T].rearrange("p n s -> p (n s)")))
                dve.tensor_scalar(spread[0:T, 0:1], moments1[0:T, 1:2], EPS, None, ALU.add).then_inc(S["l1_var"], 1)
                dve.wait_ge(S["l1_std"], t + 1)
                link_1(dve.reciprocal(spread[0:T, 2:3], spread[0:T, 1:2]))
                dve.wait_ge(S["l1_free"], t + 1)
                dve.tensor_scalar(ynew[:, :], ysum[:, :], moments1[0:T, 0:1], spread[0:T, 2:3], ALU.subtract,
                                  ALU.mult).then_inc(S["l1_made"], 1)
                dve.wait_ge(S["l1_made"], t + 1)

            def pair(i, final):
                for b in range(2):
                    t = 2 * i + b
                    if not (final and b):
                        split_lo(t + 1, 1 - b, i + 1 + b)
                    link_1, m = linker(L1_LINKS, t)
                    rows1(t, b, link_1)
                    assert m[0] == L1_LINKS, m[0]

            L1_LINKS = 6
            split_lo(0, 0, 1)
            with dve.Fori(0, NT // 2 - 1) as i:
                pair(i, False)
            pair(NT // 2 - 1, True)


_INS = ["x", "src", "dst", "edge_weight", "L0_gnn_W", "L0_gnn_a_l", "L0_gnn_a_r", "L1_gnn_W"]


def kernel(**inputs):
    import numpy as np
    import concourse.bacc as bacc
    from concourse.bass_utils import run_bass_kernel_spmd

    nc = bacc.Bacc("TRN2", target_bir_lowering=False, num_devices=1, dynamic_dma_scratch_size=1024)
    arrays, args = {}, []
    for name in _INS:
        a = np.ascontiguousarray(inputs[name])
        arrays[f"in_{name}"] = a
        args.append(nc.dram_tensor(f"in_{name}", a.shape, mybir.dt.from_np(a.dtype), kind="ExternalInput").ap())
    out = nc.dram_tensor("out", inputs["x"].shape, mybir.dt.float32, kind="ExternalOutput").ap()
    gat_gcn_resnorm(nc, *args, out)
    r = run_bass_kernel_spmd(nc, [arrays], core_ids=[0])
    return r.results[0]["out"]
```

```python
import concourse.bass as bass
from concourse import mybir
from contextlib import ExitStack


def gat_gcn_resnorm(nc, x, src, dst, edge_weight, W0, a_l, a_r, W1, out):
    f32, f32r = mybir.dt.float32, mybir.dt.float32r
    bf16, f16, i32 = mybir.dt.bfloat16, mybir.dt.float16, mybir.dt.int32
    ALU, ACT, AX = mybir.AluOpType, mybir.ActivationFunctionType, mybir.AxisListType

    N, F = x.shape
    H, _, FH = W0.shape
    E = src.shape[0]
    T = 125
    NT = N // T
    KF = F // 128
    HALF = F // 2
    FA = FH + 1
    C = E // 128
    CB = C // T
    WD = 25
    WC = WD * NT
    WT = T // WD
    NW = N // WD
    SUBS = (13, 12)
    NS = len(SUBS)
    SUB0 = [sum(SUBS[:k]) for k in range(NS)]
    NB = 2 * NS * WT
    BATCH = 4
    PAIR = 2
    NP = 2
    CPAD = C + NP * PAIR - 1
    PARTS = 3
    R = PARTS * H
    BIG = 1.0e30
    ROUND = 12582912.0
    SLOPE = 0.2
    EPS = 1e-5
    ROUNDS_MAX = NW * NS * C
    PER_TILE = WT * NS
    SHARES = [1] * (PER_TILE - 1) + [NT - PER_TILE + 1]
    SHARE = [(sum(SHARES[:n]), sum(SHARES[:n + 1])) for n in range(PER_TILE)]
    POOL_FROM = 2
    AHEAD = 2
    PEAKS_TURN = NT - 6
    LOGITS_TURN = NT - AHEAD - 1
    assert sum(SHARES) == NT and N == NT * T and E == C * 128 and C == CB * T and NW <= 128 and WC <= 512 and sum(SUBS) == WD

    w2_dram = nc.dram_tensor("w2_dram", (NT, T, NT * T), f32, kind="Internal").ap()
    xraw_dram = nc.dram_tensor("xraw_dram", (NT, T, F), f32, kind="Internal").ap()
    range_dram = nc.dram_tensor("range_dram", (NW, 2 * NS), i32, kind="Internal").ap()
    x_t = x.rearrange("(t p) f -> t p f", p=T)
    out_t = out.rearrange("(t p) f -> t p f", p=T)

    def tile_of(dram, t):
        return dram[bass.ds(t, 1)].rearrange("o p f -> (o p) f")

    ctx = ExitStack()
    with ctx:
        def sem(name):
            return ctx.enter_context(nc.semaphore(name))

        SIZE = {f32: 4, f32r: 4, i32: 4, bf16: 2, f16: 2}
        BASE = (nc.sbuf_base + 31) // 32 * 32
        LIMIT = nc.sbuf_top - BASE

        class Region:

            def __init__(self, at):
                self.at = at

            def __call__(self, name, shape, dt=f32):
                n = SIZE[dt]
                for d in shape[1:]:
                    n *= d
                self.at = (self.at + 31) // 32 * 32
                t = nc.alloc_sbuf_tensor_at(name, shape, dt, offset=BASE + self.at)
                self.at += n
                assert self.at <= LIMIT, (name, self.at)
                return t

        every = Region(0)
        ident = every("ident", [128, 128])
        ident_b = every("ident_b", [128, 128], bf16)
        moments = every("moments", [128, NT, 2])
        rstd = every("rstd", [128, NT])
        stats = every("stats", [128, 2, 6])
        moments1 = every("moments1", [128, 2])
        spread = every("spread", [128, 3])

        l0 = Region(every.at)
        key = l0("key", [128, CPAD])
        low = l0("low", [128, CPAD])
        weight = [l0(f"weight{j}", [128, CPAD]) for j in range(PARTS)]
        ranges = l0("ranges", [1, (NT + 1) * NB], i32)
        iota = l0("iota", [128, WC], f16)
        lane = l0("lane", [128, 1])
        rng = l0("rng", [128, 8])
        rng_i = l0("rng_i", [128, 2 * NS], i32)
        elr = l0("elr", [128, NT, 2 * H])
        part_f = l0("part_f", [128, NT, 2, H])
        elc = l0("elc", [128, NT, 2, 2 * R], bf16)
        lrow = l0("lrow", [128, NT, 2, T], bf16)
        block_mask = l0("block_mask", [128, H, T], bf16)
        z = l0("z", [T, NT, H, FA])
        after_z = l0.at
        prodp = Region(after_z)
        w_hi = prodp("w_hi", [128, KF, F], f32r)
        w_lo = prodp("w_lo", [128, KF, F], f32r)
        xt = [prodp(f"xt{b}", [T, F]) for b in range(2)]
        xT_hi = [prodp(f"xT_hi{b}", [128, KF, T], f32r) for b in range(2)]
        xT_lo = [prodp(f"xT_lo{b}", [128, KF, T], f32r) for b in range(2)]
        hit = prodp("hit", [128, 2, C])
        spread_r = prodp("spread_r", [128, 2, C])
        iota_f = prodp("iota_f", [128, C])
        acol = [prodp(f"acol{n}", [128, F]) for n in range(2)]
        prod = prodp("prod", [T, F])
        prep = Region(after_z - 4 * NT * H * FA)
        raw_i = prep("raw_i", [T, 2, CB, 128], i32)
        whi_r = prep("parts_b", [T, CB, 128], bf16)
        edge = prep("edge", [T, 9, CB, 128])
        w_raw = prep("w_raw", [128, KF, F])
        assert prep.at <= after_z
        prep1 = Region(after_z + 4 * KF * F)
        diag = prep1("diag", [T, 2 * CB, T])
        ones = prep1("ones", [128, 128])
        iota_i = prep1("iota_i", [128, C], i32)
        lane_i = prep1("lane_i", [128, 1], i32)
        agg = Region(after_z)
        count = agg("count", [T, 2, NT, T])
        wsum = agg("wsum", [T, NT, T])
        absent = agg("absent", [T, NT, WD])
        reach = agg("reach", [T, H, NT, WD])
        peak = agg("peak", [T, H, T])
        small = agg("small", [128, 12, H])
        q = agg("q", [T, 2, H])
        qc = agg("qc", [T, 2, 2 * R], bf16)
        qrow = agg("qrow", [128, 2, H, T], bf16)
        e_both = [agg(f"e_both{j}", [T, 2, H * T]) for j in range(2)]
        prob = [agg(f"prob{j}", [T, H, T]) for j in range(4)]

        class Hots:

            def __init__(self, name, chunks):
                self.s = agg(f"{name}_s", [128, chunks, T], bf16)
                self.d = agg(f"{name}_d", [128, chunks, max(SUBS) * NT], bf16)
                self.w = [agg(f"{name}_w{j}", [128, chunks, T], bf16) for j in range(PARTS)]

        batch_hots = [Hots(f"batch{b}", BATCH) for b in range(2)]
        pair_hots = [Hots(f"pair{b}", PAIR) for b in range(NP)]
        xres = agg("xres", [T, F])
        xsum = agg("xsum", [T, F])

        l1 = Region(every.at)
        assert agg.at <= prodp.at - 4 * 3 * F
        sup_hi, sup_lo = [], []
        for n in range(2):
            sup_hi.append(l1(f"sup_hi{n}", [T, NT, HALF], f32r))
            second_lo = l1.at
            sup_lo.append(l1(f"sup_lo{n}", [T, NT, HALF], f32r))
        after_sup = l1.at
        l1p = Region(after_sup)
        w1_hi = l1p("w1_hi", [128, KF, HALF], f32r)
        w1_lo = l1p("w1_lo", [128, KF, HALF], f32r)
        yT_hi = [l1p(f"yT_hi{b}", [128, KF, T], f32r) for b in range(2)]
        yT_lo = [l1p(f"yT_lo{b}", [128, KF, T], f32r) for b in range(2)]
        early = Region((LIMIT - 4 * (KF * HALF + 2 * F)) // 32 * 32)
        assert agg.at <= early.at
        w1_raw = [early("w1_raw0", [128, KF, HALF]), Region(second_lo)("w1_raw1", [128, KF, HALF])]
        assert l1p.at <= early.at
        yt = [early(f"yt{b}", [T, F]) for b in range(2)]
        l1a = Region(after_sup)
        first_raw = Region((LIMIT - 4 * NT * T) // 32 * 32)
        assert l1p.at <= first_raw.at
        w2_raw = [first_raw("w2_raw0", [T, NT, T]), l1a("w2_raw1", [T, NT, T])]
        NG = 4
        GS = NT // NG
        w2_hi = [l1a(f"w2_hi{g}", [T, GS, T], f32r) for g in range(NG)]
        w2_lo = [l1a(f"w2_lo{g}", [T, GS, T], f32r) for g in range(NG)]
        yres = [l1a(f"yres{b}", [T, F]) for b in range(2)]
        ysum = l1a("ysum", [T, F])
        ynew = l1a("ynew", [T, F])
        assert l1a.at <= (LIMIT - 4 * NT * T) // 32 * 32

        ps = ctx.enter_context(nc.psum_tensor("ps", [128, 8, 512], f32))
        COUNT, WSUM, SCORE = 4, 5, 6

        EL_BANKS = (0, 1, 2, 3, SCORE)
        assert 2 * NT == 8 * len(EL_BANKS)

        def bf_view(bank):
            return ps[:, bank, :].bitcast(bf16)

        names = """edges_in weights_in attn_in const_made const_self range_out range_in
            edge_made edge_turned edge_kept diag_made range_spread w_hi_made w_lo_made elr_made
            x0_in x1_in turned xT_hi_made xT_lo_made product z_kept z_kept_act elc_made el_turned lrow_made
            batch_s_made batch_made batch_w_act batch_w_pool batch_used pair_s_made pair_made pair_w_act pair_w_pool pair_used bank_kept absent_made reach_made peak_part wsum_free w2_out
            peak_made peak_turned top_made q_made q_turned qrow_made scores exp_done emax_done prob_done
            agg_done agg_kept res_in res_free xsum_made xsum_out xsum_free chain chain_pool
            rstd_var rstd_std w1_in0 w1_in1 w1_hi_made w1_split
            y0_in y1_in y_norm y_turned yT_hi_made yT_lo_made y_product sup_hi_made sup_lo_made
            w2_in0 w2_in1 res1_in0 res1_in1 w2_hi_made w2_lo_made group_used l1_agg_kept l1_var l1_std l1_made l1_out
            l1_free""".split()
        S = {n: sem(n) for n in names}

        block = ctx.enter_context(nc.Block())

        def load_bounds(eng, regs, tile):
            eng.load(regs, ranges[0:1, bass.ds(NB * tile, NB)])

        def first_of(eng, regs, n):
            return eng.snap(regs[2 * n], min_val=0, max_val=C - BATCH)

        def end_of(eng, regs, n):
            return eng.snap(regs[2 * n + 1], min_val=0, max_val=C)

        @block.sync
        def _(sp):
            sp.dma_start(raw_i[:, 0], src.rearrange("(b r k) -> r b k", b=CB, r=T)).then_inc(S["edges_in"], 16)
            sp.dma_start(raw_i[:, 1], dst.rearrange("(b r k) -> r b k", b=CB, r=T)).then_inc(S["edges_in"], 16)
            sp.dma_start(edge[:, 0], edge_weight.rearrange("(b r k) -> r b k", b=CB, r=T)).then_inc(S["edges_in"], 16)
            for b, arrived in enumerate((S["x0_in"], S["x1_in"])):
                sp.dma_start(xt[b][:, :], x_t[b]).then_inc(arrived, 16)
            for h in range(H):
                sp.dma_start(w_raw[:, :, h * FH:(h + 1) * FH],
                             W0[h].rearrange("(k p) f -> p k f", p=128)).then_inc(S["weights_in"], 16)
            for n, a in enumerate((a_l, a_r)):
                sp.dma_start(acol[n][:, :], a.rearrange("(o h) f -> o (h f)", o=1).to_broadcast([128, F])).then_inc(S["attn_in"], 16)
            with sp.Fori(1, NT // 2) as i:
                for b, arrived in enumerate((S["x0_in"], S["x1_in"])):
                    sp.wait_ge(S["turned"], 2 * i + b - 1)
                    sp.dma_start(xt[b][:, :], tile_of(x_t, 2 * i + b)).then_inc(arrived, 16)
            sp.wait_ge(S["range_out"], 1)
            sp.dma_start(range_dram, rng_i[0:NW, :]).then_inc(S["range_in"], 16)
            sp.wait_ge(S["range_in"], 16)
            sp.dma_start(ranges[:, 0:NT * NB], range_dram.rearrange("(o w) r -> o (w r)", o=1)).then_inc(S["range_in"], 16)

            def w1_half_in(n):
                sp.dma_start(w1_raw[n][:, :, :], W1.rearrange("(k p) f -> p k f", p=128)[:, :, n * HALF:(n + 1) * HALF]).then_inc(S[f"w1_in{n}"], 16)

            sp.wait_ge(S["z_kept"], NT)
            sp.wait_ge(S["z_kept_act"], NT)

            sp.wait_ge(S["elr_made"], 1)
            w1_half_in(0)

            def weights_out(t):
                sp.wait_ge(S["bank_kept"], WT * t + WT + 1)
                sp.dma_start(tile_of(w2_dram, t), wsum.rearrange("p s d -> p (s d)")).then_inc(S["w2_out"], 16)
                sp.wait_ge(S["w2_out"], 16 * t + 16)
                sp.sem_inc(S["wsum_free"], 1)

            def rows_in_out(t):
                sp.wait_ge(S["xsum_made"], t + 1)
                sp.dma_start(tile_of(xraw_dram, t), xsum[:, :]).then_inc(S["xsum_out"], 16)
                sp.wait_ge(S["xsum_out"], 16 * t + 16)
                sp.sem_inc(S["xsum_free"], 1)

            def residual_in(t):
                sp.wait_ge(S["res_free"], t + 1)
                sp.dma_start(xres[:, :], tile_of(x_t, t)).then_inc(S["res_in"], 16)

            sp.sem_inc(S["wsum_free"], 1)
            sp.sem_inc(S["xsum_free"], 1)
            weights_out(0)
            with sp.Fori(0, NT - 1) as t:
                residual_in(t)
                weights_out(t + 1)
                rows_in_out(t)
            residual_in(NT - 1)
            for b, arrived in enumerate((S["y0_in"], S["y1_in"])):
                sp.dma_start(yt[b][:, :], tile_of(xraw_dram, b)).then_inc(arrived, 16)
            rows_in_out(NT - 1)
            sp.wait_ge(S["rstd_var"], 1)
            sp.wait_ge(S["xsum_free"], NT + 1)
            for n in range(2):
                if n:
                    w1_half_in(1)
                with sp.Fori(1 - n, NT // 2) as i:
                    for b, arrived in enumerate((S["y0_in"], S["y1_in"])):
                        sp.wait_ge(S["y_turned"], NT * n + 2 * i + b + 1)
                        sp.dma_start(yt[b][:, :], tile_of(xraw_dram, 2 * i + b)).then_inc(arrived, 16)
            arrived1 = (S["w2_in0"], S["w2_in1"])
            res_arrived1 = (S["res1_in0"], S["res1_in1"])

            def weights1_in(t, b):
                sp.dma_start(w2_raw[b].rearrange("p s d -> p (s d)"), tile_of(w2_dram, t)).then_inc(arrived1[b], 16)

            def residual1_in(t, b):
                sp.dma_start(yres[b][:, :], tile_of(xraw_dram, t)).then_inc(res_arrived1[b], 16)

            sp.wait_ge(S["y_turned"], 2 * NT + 2)
            weights1_in(0, 0)
            sp.wait_ge(S["sup_lo_made"], 2 * NT)
            sp.wait_ge(S["sup_hi_made"], 2 * NT)

            def tile_out(t):
                sp.wait_ge(S["l1_made"], t + 1)
                sp.dma_start(tile_of(out_t, t), ynew[:, :]).then_inc(S["l1_out"], 16)
                sp.wait_ge(S["l1_out"], 16 * t + 16)
                sp.sem_inc(S["l1_free"], 1)

            sp.sem_inc(S["l1_free"], 1)
            weights1_in(1, 1)
            for b in range(2):
                residual1_in(b, b)
            with sp.Fori(0, NT // 2 - 1) as i:
                for b in range(2):
                    sp.wait_ge(S["l1_agg_kept"], 2 * i + b + 3)
                    weights1_in(2 * i + b + 2, b)
                    residual1_in(2 * i + b + 2, b)
                    tile_out(2 * i + b)
            for b in range(2):
                tile_out(NT - 2 + b)
            sp.wait_ge(S["l1_out"], 16 * NT)

        @block.gpsimd
        def _(pool):
            n = [0]

            def link(ins):
                n[0] += 1
                ins.then_inc(S["const_self"], 1)
                pool.wait_ge(S["const_self"], n[0])

            link(pool.iota(iota_i[:], pattern=[[1, C]], base=0, channel_multiplier=0))
            link(pool.iota(lane_i[:], pattern=[[0, 1]], base=0, channel_multiplier=1))
            link(pool.tensor_copy(iota_f[:], iota_i[:]))
            link(pool.tensor_copy(iota[:], iota_i[:, 0:WC]))
            link(pool.tensor_copy(lane[:], lane_i[:]))
            link(pool.memset(ident[:], 0.0))
            link(pool.affine_select(out=ident[:], in_=ident[:], compare_op=ALU.not_equal, fill=1.0,
                                    base=0, pattern=[[-1, 128]], channel_multiplier=1))
            link(pool.tensor_copy(ident_b[:], ident[:]))
            link(pool.memset(ones[:], 1.0))
            link(pool.memset(block_mask[:], 0.0))
            for j in range(2 * PARTS):
                link(pool.affine_select(out=block_mask[:], in_=block_mask[:], compare_op=ALU.not_equal, fill=1.0,
                                        base=-j * H, pattern=[[-1, H], [0, T]], channel_multiplier=1))
            link(pool.memset(elc[:], 1.0))
            link(pool.memset(lrow[:], 0.0))
            pool.sem_inc(S["const_made"], 1)

            pool.wait_ge(S["z_kept"], NT)
            pool.wait_ge(S["z_kept_act"], NT)
            link(pool.memset(qc[:], 1.0))
            link(pool.memset(qrow[:], 0.0))
            pool.sem_inc(S["const_made"], 1)
            pool.wait_ge(S["range_in"], 32)
            pool.sem_inc(S["reach_made"], 1)
            regs = [pool.alloc_register(f"pool_bound{k}") for k in range(NB)]
            batches = pool.alloc_register("pool_batches")
            pool.reg_mov(batches, 0)
            more = pool.alloc_register("pool_more")
            pairs = pool.alloc_register("pool_pairs")
            pool.reg_mov(pairs, 0)
            links = pool.alloc_register("pool_links")
            pool.reg_mov(links, 0)
            tops = pool.alloc_register("pool_tops")
            pool.reg_mov(tops, 0)

            def weigh(hots, c, chunks, done):
                if chunks == BATCH:
                    rest = BATCH - POOL_FROM
                    pool.tensor_tensor(hots.w[1][:, POOL_FROM:, :], hots.s[:, POOL_FROM:, :],
                                       weight[1][:, bass.ds(c + POOL_FROM, rest)].rearrange("p (c o) -> p c o", o=1).to_broadcast([128, rest, T]),
                                       ALU.mult)
                pool.tensor_tensor(hots.w[2][:, :, :], hots.s[:, :, :],
                                   weight[2][:, bass.ds(c, chunks)].rearrange("p (c o) -> p c o", o=1).to_broadcast([128, chunks, T]),
                                   ALU.mult).then_inc(done, 1)

            def batch(n):
                pool.wait_ge(S["batch_s_made"], pool.snap(batches, min_val=0, max_val=NW * NS) + 1)
                pool.reg_add(batches, batches, 1)
                weigh(batch_hots[n % 2], first_of(pool, regs, n), BATCH, S["batch_w_pool"])

            def rest(n):
                pool.reg_add(more, regs[2 * n], BATCH)
                with pool.If_lt(more, regs[2 * n + 1]):
                    with pool.Fori(pool.snap(more, min_val=BATCH, max_val=C), end_of(pool, regs, n), NP * PAIR) as c:
                        for b in range(NP):
                            pool.wait_ge(S["pair_s_made"], pool.snap(pairs, min_val=0, max_val=ROUNDS_MAX) + 2)
                            pool.reg_add(pairs, pairs, 1)
                            weigh(pair_hots[b], pool.snap(c + b * PAIR, min_val=0, max_val=CPAD - PAIR), PAIR, S["pair_w_pool"])

            def reaches(a, w, half):
                pool.wait_ge(S["elr_made"], 1)
                pool.wait_ge(S["absent_made"], WT * a + w + 2)
                pool.wait_ge(S["peak_part"], 2 * (WT * a + w) + 1)
                h0, h1 = half * H // 2, (half + 1) * H // 2
                shape = [T, H // 2, NT, WD]
                pool.tensor_tensor(reach[:, h0:h1], absent.rearrange("p (o s) d -> p o s d", o=1).to_broadcast(shape),
                                   elr[0:T, :, h0:h1].rearrange("p s (h o) -> p h s o", o=1).to_broadcast(shape),
                                   ALU.add).then_inc(S["reach_made"], 1)

            def windows(a):
                for n in range(PER_TILE):
                    rest(n)
                    if n + 1 < PER_TILE:
                        batch(n + 1)
                    else:
                        load_bounds(pool, regs, a + 1)
                        batch(0)
                    if n >= NS:
                        reaches(a, n // NS - 1, n % NS)
                for half in range(2):
                    reaches(a, WT - 1, half)

            def softmax_rows(a):
                m = [0]

                before = [0]

                def go(ins):
                    before[0] += 1
                    ins.then_inc(S["chain_pool"], 1)

                def link_a(ins):
                    ins.then_inc(S["chain_pool"], 1)
                    n = before[0] + 1
                    before[0] = 0
                    m[0] += n
                    pool.wait_ge(S["chain_pool"], pool.snap(links, min_val=0, max_val=NT * POOL_LINKS) + n)
                    pool.reg_add(links, links, n)

                top, has, er = small[0:T, 0, :], small[0:T, 1, :], small[0:T, 11, :]
                link_a(pool.tensor_copy(er, elr[0:T, bass.ds(a, 1), H:2 * H].rearrange("p o h -> p (o h)")))
                go(pool.tensor_scalar(small[0:T, 10, :], er, SLOPE, None, ALU.mult))
                pool.wait_ge(S["top_made"], pool.snap(tops, min_val=0, max_val=NT) + 1)
                pool.reg_add(tops, tops, 1)
                link_a(pool.tensor_scalar(has, top, -BIG / 2, None, ALU.is_gt))
                link_a(pool.tensor_tensor(small[0:T, 2, :], top, has, ALU.mult))
                link_a(pool.tensor_tensor(small[0:T, 3, :], small[0:T, 2, :], er, ALU.add))
                go(pool.tensor_scalar(small[0:T, 4, :], small[0:T, 3, :], 0.0, 1.0 - SLOPE, ALU.max, ALU.mult))
                link_a(pool.tensor_scalar(small[0:T, 8, :], small[0:T, 3, :], SLOPE, None, ALU.mult))
                link_a(pool.tensor_tensor(small[0:T, 9, :], small[0:T, 8, :], small[0:T, 4, :], ALU.add))
                go(pool.tensor_tensor(q[:, 0, :], er, small[0:T, 9, :], ALU.subtract))
                link_a(pool.tensor_tensor(q[:, 1, :], small[0:T, 10, :], small[0:T, 9, :], ALU.subtract))
                for j in range(PARTS):
                    part = qc[:, :, j * H:(j + 1) * H]
                    link_a(pool.tensor_copy(part, q[:, :, :]))
                    if j < PARTS - 1:
                        link_a(pool.tensor_tensor(q[:, :, :], q[:, :, :], part, ALU.subtract))
                assert m[0] == POOL_LINKS, m[0]
                pool.sem_inc(S["q_made"], 1)

            POOL_LINKS = 15
            load_bounds(pool, regs, 0)
            batch(0)
            windows(0)
            softmax_rows(0)
            with pool.Fori(0, NT - 1) as t:
                windows(t + 1)
                softmax_rows(t + 1)

        def three_products(pe, to, left_hi, left_lo, right_hi, right_lo, first, last):
            pe.matmul(to, left_hi, right_hi, start=first, stop=False)
            pe.matmul(to, left_hi, right_lo, start=False, stop=False)
            return pe.matmul(to, left_lo, right_hi, start=False, stop=last)

        def turn(pe, tiles, arrived, done, t, b, turned):
            pe.wait_ge(arrived[b], done)
            for k in range(KF):
                last = pe.transpose(ps[:, k // 4, (k % 4) * T:(k % 4 + 1) * T],
                                    tiles[b][:, k * 128:(k + 1) * 128], ident[0:T, 0:T])
            last.then_inc(turned, 1)

        @block.tensor
        def _(pe):
            pe.wait_ge(S["const_made"], 1)
            pe.wait_ge(S["edge_made"], 1)
            for a in range(2 + PARTS):
                if a == 4:
                    pe.wait_ge(S["edge_kept"], 1)
                for b in range(CB):
                    last = pe.transpose(ps[:, 2 * (a % 4) + b // 3, (b % 3) * T:(b % 3 + 1) * T], edge[:, 1 + a, b, :], ident[0:T, 0:T])
                last.then_inc(S["edge_turned"], 1)
            pe.wait_ge(S["diag_made"], 1)
            for a in range(2):
                for b in range(CB):
                    last = pe.matmul(ps[0:T, 2 + 2 * a + b // 3, (b % 3) * T:(b % 3 + 1) * T], ones[0:T, 0:T],
                                     diag[:, a * CB + b, :], start=True, stop=True)
            last.then_inc(S["range_spread"], 1)

            xs = (S["x0_in"], S["x1_in"])
            pe.wait_ge(S["edge_kept"], 2)
            turn(pe, xt, xs, 16, 0, 0, S["turned"])

            def features(i, final):
                for b in range(2):
                    t = 2 * i + b
                    pe.wait_ge(S["xT_lo_made"], t + 1)
                    if not (final and b):
                        turn(pe, xt, xs, 16 * i + 16 + 16 * b, t + 1, 1 - b, S["turned"])
                    for n in range(2):
                        pe.wait_ge(S["w_lo_made"], n + 1)
                        at = slice(n * HALF, (n + 1) * HALF)
                        for k in range(KF):
                            last = three_products(pe, ps[0:T, 2 + 2 * b + n, :], xT_hi[b][:, k, :], xT_lo[b][:, k, :],
                                                  w_hi[:, k, at], w_lo[:, k, at], k == 0, k == KF - 1)
                    last.then_inc(S["product"], 1)

            with pe.Fori(0, NT // 2 - 1) as i:
                features(i, False)
            features(NT // 2 - 1, True)
            pe.wait_ge(S["z_kept"], NT)
            pe.wait_ge(S["z_kept_act"], NT)
            pe.wait_ge(S["const_made"], 2)
            pe.wait_ge(S["range_in"], 32)

            pe.sem_inc(S["batch_used"], 2)
            pe.sem_inc(S["pair_used"], NP)
            pe.sem_inc(S["agg_done"], 4)
            regs = [pe.alloc_register(f"pe_bound{k}") for k in range(NB)]
            more = pe.alloc_register("pe_more")
            pairs = pe.alloc_register("pe_pairs")
            pe.reg_mov(pairs, 0)

            def count_chunks(hots, chunks, k, value, sems, first):
                made, w_act, w_pool, used = sems
                at = slice(SUB0[k] * NT, (SUB0[k] + SUBS[k]) * NT)
                pe.wait_ge(S[made], value)
                for c in range(chunks):
                    pe.matmul(ps[0:T, COUNT, at], hots.s[:, c, :], hots.d[:, c, 0:SUBS[k] * NT],
                              start=first and c == 0, stop=True, skip_group_check=True)
                pe.wait_ge(S[w_act], value)
                pe.wait_ge(S[w_pool], value)
                for c in range(chunks):
                    for j in range(PARTS):
                        last = pe.matmul(ps[0:T, WSUM, at], hots.w[j][:, c, :], hots.d[:, c, 0:SUBS[k] * NT],
                                         start=first and c == 0 and j == 0, stop=True, skip_group_check=True)
                last.then_inc(S[used], 1)

            def part_of_window(a, n):
                if n % NS == 0:
                    pe.wait_ge(S["bank_kept"], WT * a + n // NS + 1)
                count_chunks(batch_hots[n % 2], BATCH, n % NS, PER_TILE * a + n + 1,
                             ("batch_made", "batch_w_act", "batch_w_pool", "batch_used"), True)
                pe.reg_add(more, regs[2 * n], BATCH)
                with pe.If_lt(more, regs[2 * n + 1]):
                    with pe.Fori(pe.snap(more, min_val=BATCH, max_val=C), end_of(pe, regs, n), NP * PAIR):
                        for b in range(NP):
                            count_chunks(pair_hots[b], PAIR, n % NS, pe.snap(pairs, min_val=0, max_val=ROUNDS_MAX) + 2,
                                         ("pair_made", "pair_w_act", "pair_w_pool", "pair_used"), False)
                            pe.reg_add(pairs, pairs, 1)

            def turn_peaks(a):
                pe.wait_ge(S["peak_made"], a + 1)
                pe.wait_ge(S["bank_kept"], WT * a + WT + 1)
                for h in range(H):
                    last = pe.transpose(ps[0:T, COUNT, h * T:(h + 1) * T], peak[:, h, :], ident[0:T, 0:T])
                last.then_inc(S["peak_turned"], 1)

            def turn_logits(a):
                pe.wait_ge(S["q_made"], a + 1)
                for v in range(2):
                    last = pe.transpose(bf_view(WSUM)[0:2 * R, v * 128:v * 128 + T], qc[:, v, :], ident_b[0:T, 0:T])
                last.then_inc(S["q_turned"], 1)

            def scores(t, s):
                pe.wait_ge(S["exp_done"], NT * t + s + 1)
                for v in range(2):
                    last = pe.matmul(ps[0:T, SCORE + v, 0:H * T], lrow[:, s, v, :],
                                     qrow[:, v].rearrange("p h d -> p (h d)"), start=True, stop=True)
                last.then_inc(S["scores"], 1)

            def attend(t, s):
                pe.wait_ge(S["prob_done"], NT * t + s + 3)
                for h in range(H):
                    if s == 0:
                        pe.wait_ge(S["agg_kept"], H * t + h + 1)
                    last = pe.matmul(ps[0:T, h, 0:FA], prob[s % 4][:, h, :], z[:, s, h, :],
                                     start=(s == 0), stop=(s == NT - 1))
                last.then_inc(S["agg_done"], 1)

            def tile(t, counting):
                for n, (s0, s1) in enumerate(SHARE):
                    if counting:
                        part_of_window(t + 1, n)
                    for s in range(s0, s1):
                        if s + AHEAD < NT:
                            scores(t, s + AHEAD)
                        elif counting:
                            if s + AHEAD == NT:
                                pe.wait_ge(S["qrow_made"], t + 2)
                            scores(t + 1, s + AHEAD - NT)
                        if counting and s == PEAKS_TURN:
                            turn_peaks(t + 1)
                        if counting and s == LOGITS_TURN:
                            turn_logits(t + 1)
                        attend(t, s)

            load_bounds(pe, regs, 0)
            for n in range(PER_TILE):
                part_of_window(0, n)
                if n == 3:
                    pe.wait_ge(S["elc_made"], 1)
                    for m in range(2 * NT):
                        last = pe.transpose(bf_view(EL_BANKS[m // 8])[0:2 * R, (m % 8) * 128:(m % 8) * 128 + T],
                                            elc[0:T, m // 2, m % 2, :], ident_b[0:T, 0:T])
                    last.then_inc(S["el_turned"], 1)
            turn_peaks(0)
            turn_logits(0)
            pe.wait_ge(S["lrow_made"], 1)
            pe.wait_ge(S["qrow_made"], 1)
            for s in range(AHEAD):
                scores(0, s)
            with pe.Fori(0, NT - 1) as t:
                load_bounds(pe, regs, t + 1)
                tile(t, True)
            tile(NT - 1, False)

            pe.wait_ge(S["agg_kept"], H * NT + H)
            ys = (S["y0_in"], S["y1_in"])
            pe.sem_inc(S["y_turned"], 2)
            for n in range(2):
                pe.wait_ge(S["y_norm"], NT * n + 1)
                turn(pe, yt, ys, 16 * (NT // 2) * n + 16, 0, 0, S["y_turned"])

                def features1(i, final):
                    for b in range(2):
                        t = 2 * i + b
                        pe.wait_ge(S["yT_lo_made"], NT * n + t + 1)
                        if not (final and b):
                            pe.wait_ge(S["y_norm"], NT * n + t + 2)
                            turn(pe, yt, ys, 16 * (NT // 2) * n + 16 * i + 16 + 16 * b, t + 1, 1 - b, S["y_turned"])
                        for k in range(KF):
                            last = three_products(pe, ps[0:T, 2 + b, :], yT_hi[b][:, k, :], yT_lo[b][:, k, :],
                                                  w1_hi[:, k, :], w1_lo[:, k, :], k == 0, k == KF - 1)
                        last.then_inc(S["y_product"], 1)

                with pe.Fori(0, NT // 2 - 1) as i:
                    features1(i, False)
                features1(NT // 2 - 1, True)

            pe.wait_ge(S["sup_lo_made"], 2 * NT)
            pe.sem_inc(S["group_used"], NG)
            with pe.Fori(0, NT // 2) as i:
                for b in range(2):
                    t = 2 * i + b
                    pe.wait_ge(S["l1_agg_kept"], t + 1)
                    for g in range(NG):
                        pe.wait_ge(S["w2_lo_made"], NG * t + g + 1)
                        for s in range(GS):
                            for n in range(2):
                                last = three_products(pe, ps[0:T, 2 * b + n, :], w2_hi[g][:, s, :], w2_lo[g][:, s, :],
                                                      sup_hi[n][:, GS * g + s, :], sup_lo[n][:, GS * g + s, :],
                                                      g == 0 and s == 0, g == NG - 1 and s == GS - 1)
                        last.then_inc(S["group_used"], 1)

        @block.scalar
        def _(act):
            def turned_hi(turned, t, xT, made):
                act.wait_ge(turned, t)
                act.activation(xT.rearrange("p (a k) n -> p a (k n)", a=2), ps[:, 0:2, 0:KF // 2 * T], ACT.Copy).then_inc(made, 1)

            act.wait_ge(S["weights_in"], 16 * H)
            for n in range(2):
                at = slice(n * HALF, (n + 1) * HALF)
                act.activation(w_hi[:, :, at], w_raw[:, :, at], ACT.Copy).then_inc(S["w_hi_made"], 1)
            turned_hi(S["turned"], 1, xT_hi[0], S["xT_hi_made"])

            def features(i, final):
                for b in range(2):
                    t = 2 * i + b
                    if not (final and b):
                        turned_hi(S["turned"], t + 2, xT_hi[1 - b], S["xT_hi_made"])
                    act.wait_ge(S["product"], t + 1)
                    act.activation(z[:, bass.ds(t, 1), H // 2:, 0:FH].rearrange("p o h f -> p (o h) f"),
                                   ps[0:T, 3 + 2 * b, :].rearrange("p (h f) -> p h f", h=H // 2), ACT.Copy).then_inc(S["z_kept_act"], 1)

            with act.Fori(0, NT // 2 - 1) as i:
                features(i, False)
            features(NT // 2 - 1, True)

            act.wait_ge(S["z_kept"], NT)
            act.wait_ge(S["range_in"], 32)
            act.sem_inc(S["bank_kept"], 1)
            act.sem_inc(S["exp_done"], 1)
            regs = [act.alloc_register(f"act_bound{k}") for k in range(NB)]
            more = act.alloc_register("act_more")
            pairs = act.alloc_register("act_pairs")
            act.reg_mov(pairs, 0)

            def weigh(hots, c, chunks, done):
                for i in range(chunks):
                    for j in range(2):
                        if (chunks == PAIR and i == 0 and j == 0) or (chunks == BATCH and i >= POOL_FROM and j == 1):
                            continue
                        last = act.activation(hots.w[j][:, i, :], hots.s[:, i, :], ACT.Copy, scale=weight[j][:, bass.ds(c + i, 1)])
                last.then_inc(done, 1)

            def batch(a, n):
                act.wait_ge(S["batch_s_made"], PER_TILE * a + n + 1)
                weigh(batch_hots[n % 2], first_of(act, regs, n), BATCH, S["batch_w_act"])

            def rest(n):
                act.reg_add(more, regs[2 * n], BATCH)
                with act.If_lt(more, regs[2 * n + 1]):
                    with act.Fori(act.snap(more, min_val=BATCH, max_val=C), end_of(act, regs, n), NP * PAIR) as c:
                        for b in range(NP):
                            act.wait_ge(S["pair_s_made"], act.snap(pairs, min_val=0, max_val=ROUNDS_MAX) + 2)
                            weigh(pair_hots[b], c + b * PAIR, PAIR, S["pair_w_act"])
                            act.reg_add(pairs, pairs, 1)

            def keep_banks(a, par, w):
                if w == 0:
                    act.wait_ge(S["wsum_free"], a + 1)
                act.wait_ge(S["batch_used"], PER_TILE * a + NS * w + NS + 2)
                act.wait_ge(S["pair_used"], act.snap(pairs, min_val=0, max_val=ROUNDS_MAX) + NP)
                at = slice(w * WD, (w + 1) * WD)
                act.activation(count[:, bass.ds(par, 1), :, at].rearrange("p o s d -> p d (o s)"),
                               ps[0:T, COUNT, 0:WC].rearrange("p (d s) -> p d s", d=WD), ACT.Copy)
                act.activation(wsum[:, :, at].rearrange("p s d -> p d s"),
                               ps[0:T, WSUM, 0:WC].rearrange("p (d s) -> p d s", d=WD), ACT.Copy).then_inc(S["bank_kept"], 1)

            def exps(t, s):
                act.wait_ge(S["scores"], NT * t + s + 1)
                act.wait_ge(S["prob_done"], NT * t + s + 1)
                act.activation(e_both[s % 2][:, :, :], ps[0:T, SCORE:SCORE + 2, 0:H * T], ACT.Exp).then_inc(S["exp_done"], 1)

            def count_ahead(a, n, keep=False):
                rest(n)
                if keep:
                    keep_banks(a, a & 1, n // NS)
                if n + 1 < PER_TILE:
                    batch(a, n + 1)
                else:
                    load_bounds(act, regs, a + 1)
                    batch(a + 1, 0)

            def tile(t, counting):
                for n, (s0, s1) in enumerate(SHARE):
                    if counting:
                        count_ahead(t + 1, n, keep=n == NS - 1)
                    for s in range(s0, s1):
                        if s + AHEAD < NT:
                            exps(t, s + AHEAD)
                        elif counting:
                            exps(t + 1, s + AHEAD - NT)
                        if counting and s == s0 and n % NS == NS - 1 and n != NS - 1:
                            keep_banks(t + 1, (t + 1) & 1, n // NS)

            load_bounds(act, regs, 0)
            batch(0, 0)
            for n in range(PER_TILE):
                count_ahead(0, n)
                if n % NS == NS - 1:
                    keep_banks(0, 0, n // NS)
            for s in range(AHEAD):
                exps(0, s)
            with act.Fori(0, NT - 1) as t:
                tile(t, True)
            tile(NT - 1, False)

            act.wait_ge(S["rstd_var"], 1)
            act.activation(rstd[0:T, :], rstd[0:T, :], ACT.Sqrt).then_inc(S["rstd_std"], 1)
            for n in range(2):
                act.wait_ge(S[f"w1_in{n}"], 16)
                if n == 0:
                    act.wait_ge(S["agg_kept"], H * NT + H)
                else:
                    act.wait_ge(S["y_product"], NT)
                for m in range(2):
                    at = slice(m * KF // 2, (m + 1) * KF // 2)
                    act.activation(w1_hi[:, at, :], w1_raw[n][:, at, :], ACT.Copy).then_inc(S["w1_hi_made"], 1)
                act.wait_ge(S["w1_split"], 2 * n + 2)
                turned_hi(S["y_turned"], NT * n + 3, yT_hi[0], S["yT_hi_made"])

                def features1(i, final):
                    for b in range(2):
                        t = 2 * i + b
                        if not (final and b):
                            turned_hi(S["y_turned"], NT * n + t + 4, yT_hi[1 - b], S["yT_hi_made"])
                        act.wait_ge(S["y_product"], NT * n + t + 1)
                        act.activation(sup_hi[n][:, bass.ds(t, 1), :].rearrange("p o f -> p (o f)"),
                                       ps[0:T, 2 + b, :], ACT.Copy).then_inc(S["sup_hi_made"], 1)

                with act.Fori(0, NT // 2 - 1) as i:
                    features1(i, False)
                features1(NT // 2 - 1, True)
            act.wait_ge(S["sup_lo_made"], 2 * NT)
            arrived1 = (S["w2_in0"], S["w2_in1"])

            def split_hi(t, b, arrivals):
                act.wait_ge(arrived1[b], 16 * arrivals)
                for g in range(NG):
                    act.wait_ge(S["group_used"], NG * t + g + 1)
                    act.activation(w2_hi[g][:, :, :], w2_raw[b][:, GS * g:GS * g + GS, :], ACT.Copy).then_inc(S["w2_hi_made"], 1)

            def pair(i, final):
                for b in range(2):
                    t = 2 * i + b
                    if not (final and b):
                        split_hi(t + 1, 1 - b, i + 1 + b)
                    act.wait_ge(S["l1_var"], t + 1)
                    act.activation(spread[0:T, 1:2], spread[0:T, 0:1], ACT.Sqrt).then_inc(S["l1_std"], 1)

            split_hi(0, 0, 1)
            with act.Fori(0, NT // 2 - 1) as i:
                pair(i, False)
            pair(NT // 2 - 1, True)

        @block.vector
        def _(dve):
            n_chain = [0]

            def link(ins):
                n_chain[0] += 1
                ins.then_inc(S["chain"], 1)
                dve.wait_ge(S["chain"], n_chain[0])

            def linker(per, index):
                base, m = n_chain[0], [0]

                def link_in(ins):
                    m[0] += 1
                    ins.then_inc(S["chain"], 1)
                    dve.wait_ge(S["chain"], index * per + base + m[0])
                return link_in, m

            dve.wait_ge(S["edges_in"], 48)
            srcf, dstf, hi_s = edge[:, 6], edge[:, 7], edge[:, 8]
            e_low, e_key, w_in = edge[:, 1], edge[:, 2], edge[:, 0]
            link(dve.tensor_copy(srcf, raw_i[:, 0]))
            link(dve.tensor_copy(dstf, raw_i[:, 1]))
            link(dve.tensor_scalar(hi_s, srcf, -(T // 2) * 1.0, 1.0 / T, ALU.add, ALU.mult))
            link(dve.tensor_scalar(hi_s, hi_s, ROUND, ROUND, ALU.add, ALU.subtract))
            link(dve.scalar_tensor_tensor(e_low, hi_s, -1.0 * T, srcf, ALU.mult, ALU.add))
            link(dve.scalar_tensor_tensor(e_key, dstf, 1.0 * NT, hi_s, ALU.mult, ALU.add))
            for j in range(PARTS):
                link(dve.tensor_copy(whi_r[:, :, :], w_in))
                link(dve.tensor_copy(edge[:, 3 + j], whi_r[:, :, :]))
                if j < PARTS - 1:
                    link(dve.tensor_tensor(w_in, w_in, edge[:, 3 + j], ALU.subtract))
            dve.sem_inc(S["edge_made"], 1)
            dve.wait_ge(S["const_made"], 1)
            link(dve.tensor_reduce(hit[0:T, 0, 0:CB], dstf, AX.X, ALU.min))
            link(dve.tensor_reduce(hit[0:T, 1, 0:CB], dstf, AX.X, ALU.max))
            for a in range(2):
                for b in range(CB):
                    link(dve.tensor_scalar(diag[:, a * CB + b, :], ident[0:T, 0:T], hit[0:T, a, b:b + 1], None, ALU.mult))
            for a, to in enumerate((low, key, *weight)):
                dve.wait_ge(S["edge_turned"], a + 1)
                for n in range(2):
                    width = min(3, CB - 3 * n) * T
                    link(dve.tensor_copy(to[:, 3 * n * T:3 * n * T + width], ps[:, 2 * (a % 4) + n, 0:width]))
                if a == 3:
                    dve.sem_inc(S["edge_kept"], 1)
                    dve.sem_inc(S["diag_made"], 1)
            dve.memset(ranges[:, NT * NB:(NT + 1) * NB], 0)
            for to, value in ((low, 0.0), (key, -1.0e6), *((to, 0.0) for to in weight)):
                dve.memset(to[:, C:CPAD], value)
            dve.wait_ge(S["range_spread"], 1)
            for a in range(2):
                for n in range(2):
                    width = min(3, CB - 3 * n) * T
                    link(dve.tensor_copy(spread_r[0:NW, a, 3 * n * T:3 * n * T + width], ps[0:NW, 2 + 2 * a + n, 0:width]))
            dve.sem_inc(S["edge_kept"], 1)

            def turned_lo(hi_made, value, xT_h, xT_l, made):
                dve.wait_ge(hi_made, value)
                dve.tensor_tensor(xT_l.rearrange("p (a k) n -> p a (k n)", a=2), ps[:, 0:2, 0:KF // 2 * T],
                                  xT_h.rearrange("p (a k) n -> p a (k n)", a=2).bitcast(f32), ALU.subtract).then_inc(made, 1)

            for n in range(2):
                at = slice(n * HALF, (n + 1) * HALF)
                dve.wait_ge(S["w_hi_made"], n + 1)
                dve.tensor_tensor(w_lo[:, :, at], w_raw[:, :, at], w_hi[:, :, at].bitcast(f32), ALU.subtract).then_inc(S["w_lo_made"], 1)
                if n == 0:
                    turned_lo(S["xT_hi_made"], 1, xT_hi[0], xT_lo[0], S["xT_lo_made"])
            dve.wait_ge(S["w_lo_made"], 2)
            dve.memset(z[:, :, :, FH:FA], 1.0)
            dve.wait_ge(S["attn_in"], 32)

            def find_ranges():
                for k in range(NS):
                    lo, hi = rng[0:NW, 0:1], rng[0:NW, 1:2]
                    link(dve.tensor_scalar(lo, lane[0:NW, :], 1.0 * WD, 1.0 * SUB0[k], ALU.mult, ALU.add))
                    link(dve.tensor_scalar(hi, lane[0:NW, :], 1.0 * WD, SUB0[k] + SUBS[k] - 1.0, ALU.mult, ALU.add))
                    link(dve.tensor_scalar(hit[0:NW, 0], spread_r[0:NW, 1], lo, None, ALU.is_ge))
                    link(dve.scalar_tensor_tensor(hit[0:NW, 1], spread_r[0:NW, 0], hi, hit[0:NW, 0], ALU.is_le, ALU.mult))
                    link(dve.scalar_tensor_tensor(hit[0:NW, 0], iota_f[0:NW, 0:C], 1.0, hit[0:NW, 1], ALU.add, ALU.mult))
                    link(dve.tensor_reduce(rng[0:NW, 2:3], hit[0:NW, 0], AX.X, ALU.max))
                    link(dve.tensor_scalar(hit[0:NW, 0], iota_f[0:NW, 0:C], -1.0, 1.0 * C, ALU.mult, ALU.add))
                    link(dve.tensor_tensor(hit[0:NW, 0], hit[0:NW, 0], hit[0:NW, 1], ALU.mult))
                    link(dve.tensor_reduce(rng[0:NW, 3:4], hit[0:NW, 0], AX.X, ALU.max))
                    link(dve.tensor_scalar(rng[0:NW, 4:5], rng[0:NW, 3:4], -1.0, 1.0 * C, ALU.mult, ALU.add))
                    link(dve.tensor_scalar(rng[0:NW, 5:6], rng[0:NW, 4:5], 1.0 * (C - BATCH), None, ALU.min))
                    link(dve.tensor_scalar(rng[0:NW, 6:7], rng[0:NW, 5:6], 1.0 * BATCH, None, ALU.add))
                    link(dve.tensor_tensor(rng[0:NW, 6:7], rng[0:NW, 6:7], rng[0:NW, 2:3], ALU.max))
                    link(dve.tensor_copy(rng_i[0:NW, 2 * k:2 * k + 2], rng[0:NW, 5:7]))
                dve.sem_inc(S["range_out"], 1)

            def features(i, link_i, begin=False, final=False):
                for b in range(2):
                    t = 2 * i + b
                    if not (final and b):
                        turned_lo(S["xT_hi_made"], t + 2, xT_hi[1 - b], xT_lo[1 - b], S["xT_lo_made"])
                    if begin and b == 1:
                        find_ranges()
                    dve.wait_ge(S["product"], t + 1)
                    dve.tensor_copy(z[:, bass.ds(t, 1), 0:H // 2, 0:FH].rearrange("p o h f -> p (o h) f"),
                                    ps[0:T, 2 + 2 * b, :].rearrange("p (h f) -> p h f", h=H // 2)).then_inc(S["z_kept"], 1)
                    if not (final and b):
                        el_er(t, link_i)

            def el_er(t, link_i):
                z_t = z[:, bass.ds(t, 1), :, 0:FH].rearrange("p o h f -> p (o h) f")
                dve.wait_ge(S["z_kept"], t + 1)
                dve.wait_ge(S["z_kept_act"], t + 1)
                for n in range(2):
                    link_i(dve.tensor_tensor(prod.rearrange("p (h f) -> p h f", h=H), z_t,
                                             acol[n][0:T].rearrange("p (h f) -> p h f", h=H), ALU.mult))
                    link_i(dve.tensor_reduce(elr[0:T, bass.ds(t, 1), n * H:(n + 1) * H].rearrange("p o h -> p (o h)"),
                                             prod.rearrange("p (h f) -> p h f", h=H), AX.X, ALU.add))

            EL_LINKS = 8
            features(0, link, begin=True)
            with dve.Fori(1, NT // 2 - 1) as i:
                link_i, m = linker(EL_LINKS, i - 1)
                features(i, link_i)
            assert m[0] == EL_LINKS, m[0]
            n_chain[0] += EL_LINKS * (NT // 2 - 2)
            features(NT // 2 - 1, link, final=True)

            dve.wait_ge(S["z_kept_act"], NT)
            dve.wait_ge(S["const_made"], 2)
            dve.wait_ge(S["range_in"], 32)
            dve.sem_inc(S["absent_made"], 1)
            dve.sem_inc(S["peak_part"], 1)
            dve.sem_inc(S["res_free"], 1)
            dve.sem_inc(S["agg_kept"], H)
            for signal in ("pair_s_made", "pair_made", "pair_w_act", "pair_w_pool"):
                dve.sem_inc(S[signal], 1)
            dve.sem_inc(S["prob_done"], 2)
            dve.sem_inc(S["emax_done"], 2)
            regs = [dve.alloc_register(f"dve_bound{k}") for k in range(NB)]
            more = dve.alloc_register("dve_more")
            pairs = dve.alloc_register("dve_pairs")
            dve.reg_mov(pairs, 0)

            def make_hots(hots, c, chunks, n, done_s, done):
                w, k = n // NS, n % NS
                for i in range(chunks):
                    last = dve.tensor_scalar(hots.s[:, i, :], iota[:, 0:T], low[:, bass.ds(c + i, 1)], None, ALU.is_equal)
                last.then_inc(done_s, 1)
                if chunks == PAIR:
                    dve.tensor_scalar(hots.w[0][:, 0, :], iota[:, 0:T], low[:, bass.ds(c, 1)], weight[0][:, bass.ds(c, 1)],
                                      ALU.is_equal, ALU.mult)
                for i in range(chunks):
                    last = dve.tensor_scalar(hots.d[:, i, 0:SUBS[k] * NT], iota[:, 0:SUBS[k] * NT],
                                             1.0 * (w * WD + SUB0[k]) * NT, key[:, bass.ds(c + i, 1)], ALU.add, ALU.is_equal)
                last.then_inc(done, 1)

            def batch(a, n):
                dve.wait_ge(S["batch_used"], PER_TILE * a + n + 1)
                make_hots(batch_hots[n % 2], first_of(dve, regs, n), BATCH, n, S["batch_s_made"], S["batch_made"])

            def rest(n):
                dve.reg_add(more, regs[2 * n], BATCH)
                with dve.If_lt(more, regs[2 * n + 1]):
                    with dve.Fori(dve.snap(more, min_val=BATCH, max_val=C), end_of(dve, regs, n), NP * PAIR) as c:
                        for b in range(NP):
                            dve.wait_ge(S["pair_used"], dve.snap(pairs, min_val=0, max_val=ROUNDS_MAX) + 1)
                            make_hots(pair_hots[b], c + b * PAIR, PAIR, n, S["pair_s_made"], S["pair_made"])
                            dve.reg_add(pairs, pairs, 1)

            def count_ahead(a, n, link_t):
                rest(n)
                if n + 1 < PER_TILE:
                    batch(a, n + 1)
                else:
                    dve.wait_ge(S["batch_made"], PER_TILE * a + PER_TILE)
                    dve.wait_ge(S["pair_made"], dve.snap(pairs, min_val=0, max_val=ROUNDS_MAX) + 1)
                    link_t(dve.tensor_scalar(key[:, 0:C], key[:, 0:C], -1.0 * T * NT, None, ALU.add))
                    load_bounds(dve, regs, a + 1)
                    batch(a + 1, 0)

            def no_edge(a, par, w):
                dve.wait_ge(S["bank_kept"], WT * a + w + 2)
                dve.wait_ge(S["reach_made"], 2 * (WT * a + w) + 1)
                dve.tensor_scalar(absent[:, :, :], count[:, bass.ds(par, 1), :, w * WD:(w + 1) * WD].rearrange("p o s d -> p (o s) d"), 0.0, -BIG,
                                  ALU.is_equal, ALU.mult).then_inc(S["absent_made"], 1)

            def peaks(a, w, half):
                dve.wait_ge(S["reach_made"], 2 * (WT * a + w) + half + 2)
                h0, h1 = half * H // 2, (half + 1) * H // 2
                dve.tensor_reduce(peak[:, h0:h1, w * WD:(w + 1) * WD], reach[:, h0:h1].rearrange("p h s d -> p h d s"), AX.X,
                                  ALU.max).then_inc(S["peak_part"], 1)
                if w == WT - 1 and half:
                    dve.wait_ge(S["peak_part"], 2 * (WT * a + WT) + 1)
                    dve.sem_inc(S["peak_made"], 1)

            def top(a):
                dve.wait_ge(S["peak_turned"], a + 1)
                dve.tensor_reduce(small[0:T, 0, :], ps[0:T, COUNT, 0:H * T].rearrange("p (h s) -> p h s", h=H), AX.X,
                                  ALU.max).then_inc(S["top_made"], 1)

            def logits(a):
                dve.wait_ge(S["q_turned"], a + 1)
                for v in range(2):
                    last = dve.tensor_tensor(qrow[0:2 * R, v],
                                             bf_view(WSUM)[0:2 * R, v * 128:v * 128 + T].rearrange("p (o n) -> p o n", o=1).to_broadcast([2 * R, H, T]),
                                             block_mask[0:2 * R], ALU.mult)
                last.then_inc(S["qrow_made"], 1)

            def larger(t, s):
                dve.wait_ge(S["exp_done"], NT * t + s + 2)
                dve.tensor_tensor(e_both[s % 2][:, 0, :], e_both[s % 2][:, 0, :], e_both[s % 2][:, 1, :], ALU.max).then_inc(S["emax_done"], 1)

            def probs(t, par, s):
                larger(t, s)
                dve.wait_ge(S["emax_done"], NT * t + s + 3)
                dve.wait_ge(S["agg_done"], NT * t + s + 1)
                dve.scalar_tensor_tensor(prob[s % 4][:, :, :], e_both[s % 2][:, 0, :].rearrange("p (h d) -> p h d", h=H), 1.0,
                                         count[:, bass.ds(par, 1), s, :].to_broadcast([T, H, T]),
                                         ALU.min, ALU.mult).then_inc(S["prob_done"], 1)

            def rows(t, link_t):
                sums = ps[0:T, 0:H, FH:FA].rearrange("p h o -> p (h o)")
                dve.wait_ge(S["agg_done"], NT * t + NT + 4)
                link_t(dve.tensor_scalar(small[0:T, 5, :], sums, 0.0, None, ALU.is_equal))
                link_t(dve.tensor_tensor(small[0:T, 6, :], small[0:T, 5, :], sums, ALU.add))
                link_t(dve.reciprocal(small[0:T, 7, :], small[0:T, 6, :]))
                dve.wait_ge(S["res_in"], 16 * t + 16)
                dve.wait_ge(S["xsum_free"], t + 1)
                for h in range(H):
                    last = dve.scalar_tensor_tensor(xsum[:, h * FH:(h + 1) * FH], ps[0:T, h, 0:FH], small[0:T, 7, h:h + 1],
                                                    xres[:, h * FH:(h + 1) * FH], ALU.mult, ALU.add).then_inc(S["agg_kept"], 1)
                dve.wait_ge(S["agg_kept"], H * t + 2 * H)
                dve.sem_inc(S["xsum_made"], 1)

            def row_stats(t, link_t):
                for n in range(2):
                    link_t(dve.bn_stats(stats[0:T, n, :], xsum[:, n * HALF:(n + 1) * HALF]))
                dve.sem_inc(S["res_free"], 1)
                link_t(dve.bn_aggr(moments1[0:T, :], stats[0:T].rearrange("p n s -> p (n s)")))
                link_t(dve.tensor_copy(moments[0:T, bass.ds(t, 1), :].rearrange("p o m -> p (o m)"), moments1[0:T, :]))

            def window_peaks(a, n):
                v = n // NS - 1
                if n % NS == 0:
                    if v >= 1:
                        peaks(a, v - 1, 1)
                    if v >= 0:
                        no_edge(a, a & 1, v)
                elif v >= 0:
                    peaks(a, v, 0)

            def tile(t, counting, link_t, first_tile=False):
                par = t & 1
                for n, (s0, s1) in enumerate(SHARE):
                    w = n // NS
                    if counting:
                        count_ahead(t + 1, n, link_t)
                    for s in range(s0, s1):
                        if counting and s == LOGITS_TURN + 1:
                            logits(t + 1)
                        if not first_tile and s == 0:
                            rows(t - 1, link_t)
                        if s + 1 < NT:
                            probs(t, par, s + 1)
                        elif counting:
                            probs(t + 1, (t + 1) & 1, 0)
                        if not first_tile and s == PER_TILE + 1:
                            row_stats(t - 1, link_t)
                        if not counting:
                            continue
                        if s == s0:
                            window_peaks(t + 1, n)
                        if n == PER_TILE - 1:
                            if s == s0 + 1:
                                peaks(t + 1, WT - 2, 1)
                                no_edge(t + 1, (t + 1) & 1, WT - 1)
                            if s == PEAKS_TURN - 1:
                                for half in range(2):
                                    peaks(t + 1, WT - 1, half)
                            if s == PEAKS_TURN:
                                top(t + 1)

            def logit_parts():
                link(dve.tensor_copy(part_f[0:T, :, 0, :], elr[0:T, :, 0:H]))
                link(dve.tensor_scalar(part_f[0:T, :, 1, :], elr[0:T, :, 0:H], SLOPE, None, ALU.mult))
                for j in range(PARTS):
                    part = elc[0:T, :, :, R + j * H:R + (j + 1) * H]
                    link(dve.tensor_copy(part, part_f[0:T]))
                    if j < PARTS - 1:
                        link(dve.tensor_tensor(part_f[0:T], part_f[0:T], part, ALU.subtract))
                dve.sem_inc(S["elc_made"], 1)

            def keep_turned_parts():
                dve.wait_ge(S["el_turned"], 1)
                for n in range(2 * NT // 8):
                    link(dve.tensor_copy(lrow[0:2 * R, 4 * n:4 * n + 4].rearrange("p t v n -> p (t v) n"),
                                         bf_view(EL_BANKS[n])[0:2 * R, :].rearrange("p (a n) -> p a n", a=8)[:, :, 0:T]))
                dve.sem_inc(S["lrow_made"], 1)

            load_bounds(dve, regs, 0)
            batch(0, 0)
            el_er(NT - 1, link)
            dve.sem_inc(S["elr_made"], 1)
            for n in range(PER_TILE):
                count_ahead(0, n, link)
                if n == 1:
                    logit_parts()
                if n == 5:
                    keep_turned_parts()
                window_peaks(0, n)
            peaks(0, WT - 2, 1)
            no_edge(0, 0, WT - 1)
            for half in range(2):
                peaks(0, WT - 1, half)
            top(0)
            logits(0)
            probs(0, 0, 0)
            tile(0, True, link, first_tile=True)
            LINKS = 8
            with dve.Fori(1, NT - 1) as t:
                link_t, m = linker(LINKS, t - 1)
                tile(t, True, link_t)
            assert m[0] == LINKS, m[0]
            n_chain[0] += LINKS * (NT - 2)
            tile(NT - 1, False, link)
            rows(NT - 1, link)
            row_stats(NT - 1, link)

            link(dve.tensor_scalar(rstd[0:T, :], moments[0:T, :, 1], EPS, None, ALU.add))
            dve.sem_inc(S["rstd_var"], 1)
            dve.wait_ge(S["rstd_std"], 1)
            link(dve.reciprocal(rstd[0:T, :], rstd[0:T, :]))

            def normed(t):
                return moments[0:T, bass.ds(t, 1), 0:1].rearrange("p o m -> p (o m)"), rstd[0:T, bass.ds(t, 1)]

            ys = (S["y0_in"], S["y1_in"])
            for n in range(2):
                def norm(t, b, count_in):
                    dve.wait_ge(ys[b], count_in)
                    mean, r = normed(t)
                    dve.tensor_scalar(yt[b][:, :], yt[b][:, :], mean, r, ALU.subtract, ALU.mult).then_inc(S["y_norm"], 1)

                first_in = 16 * (NT // 2) * n + 16
                norm(0, 0, first_in)
                dve.wait_ge(S["xsum_free"], NT + 1)
                for m in range(2):
                    dve.wait_ge(S["w1_hi_made"], 2 * n + m + 1)
                    at = slice(m * KF // 2, (m + 1) * KF // 2)
                    dve.tensor_tensor(w1_lo[:, at, :], w1_raw[n][:, at, :], w1_hi[:, at, :].bitcast(f32),
                                      ALU.subtract).then_inc(S["w1_split"], 1)
                norm(1, 1, first_in)
                turned_lo(S["yT_hi_made"], NT * n + 1, yT_hi[0], yT_lo[0], S["yT_lo_made"])

                def features1(i, final):
                    for b in range(2):
                        t = 2 * i + b
                        if not (final and b):
                            turned_lo(S["yT_hi_made"], NT * n + t + 2, yT_hi[1 - b], yT_lo[1 - b], S["yT_lo_made"])
                        if not final:
                            norm(t + 2, b, first_in + 16 * i + 16)
                        dve.wait_ge(S["sup_hi_made"], NT * n + t + 1)
                        dve.tensor_tensor(sup_lo[n][:, bass.ds(t, 1), :].rearrange("p o f -> p (o f)"), ps[0:T, 2 + b, :],
                                          sup_hi[n][:, bass.ds(t, 1), :].rearrange("p o f -> p (o f)").bitcast(f32),
                                          ALU.subtract).then_inc(S["sup_lo_made"], 1)

                with dve.Fori(0, NT // 2 - 1) as i:
                    features1(i, False)
                features1(NT // 2 - 1, True)

            dve.sem_inc(S["l1_agg_kept"], 2)
            dve.wait_ge(S["sup_lo_made"], 2 * NT)

            arrived1 = (S["w2_in0"], S["w2_in1"])

            def split_lo(t, b, arrivals):
                dve.wait_ge(arrived1[b], 16 * arrivals)
                for g in range(NG):
                    dve.wait_ge(S["w2_hi_made"], NG * t + g + 1)
                    dve.tensor_tensor(w2_lo[g][:, :, :], w2_raw[b][:, GS * g:GS * g + GS, :], w2_hi[g][:, :, :].bitcast(f32),
                                      ALU.subtract).then_inc(S["w2_lo_made"], 1)

            def rows1(t, b, arrivals, link_1):
                dve.wait_ge((S["res1_in0"], S["res1_in1"])[b], 16 * arrivals)
                mean, r = normed(t)
                link_1(dve.tensor_scalar(yres[b][:, :], yres[b][:, :], mean, r, ALU.subtract, ALU.mult))
                dve.wait_ge(S["group_used"], NG * t + 2 * NG)
                for n in range(2):
                    last = dve.tensor_tensor(ysum[:, n * HALF:(n + 1) * HALF], ps[0:T, 2 * b + n, :],
                                             yres[b][:, n * HALF:(n + 1) * HALF], ALU.add)
                link_1(last)
                for n in range(2):
                    link_1(dve.bn_stats(stats[0:T, n, :], ysum[:, n * HALF:(n + 1) * HALF]))
                dve.sem_inc(S["l1_agg_kept"], 1)
                link_1(dve.bn_aggr(moments1[0:T, :], stats[0:T].rearrange("p n s -> p (n s)")))
                dve.tensor_scalar(spread[0:T, 0:1], moments1[0:T, 1:2], EPS, None, ALU.add).then_inc(S["l1_var"], 1)
                dve.wait_ge(S["l1_std"], t + 1)
                link_1(dve.reciprocal(spread[0:T, 2:3], spread[0:T, 1:2]))
                dve.wait_ge(S["l1_free"], t + 1)
                dve.tensor_scalar(ynew[:, :], ysum[:, :], moments1[0:T, 0:1], spread[0:T, 2:3], ALU.subtract,
                                  ALU.mult).then_inc(S["l1_made"], 1)
                dve.wait_ge(S["l1_made"], t + 1)

            def pair(i, final):
                for b in range(2):
                    t = 2 * i + b
                    if not (final and b):
                        split_lo(t + 1, 1 - b, i + 1 + b)
                    link_1, m = linker(L1_LINKS, t)
                    rows1(t, b, i + 1, link_1)
                    assert m[0] == L1_LINKS, m[0]

            L1_LINKS = 6
            split_lo(0, 0, 1)
            with dve.Fori(0, NT // 2 - 1) as i:
                pair(i, False)
            pair(NT // 2 - 1, True)


_INS = ["x", "src", "dst", "edge_weight", "L0_gnn_W", "L0_gnn_a_l", "L0_gnn_a_r", "L1_gnn_W"]


def kernel(**inputs):
    import numpy as np
    import concourse.bacc as bacc
    from concourse.bass_utils import run_bass_kernel_spmd

    nc = bacc.Bacc("TRN2", target_bir_lowering=False, num_devices=1, dynamic_dma_scratch_size=1024)
    arrays, args = {}, []
    for name in _INS:
        a = np.ascontiguousarray(inputs[name])
        arrays[f"in_{name}"] = a
        args.append(nc.dram_tensor(f"in_{name}", a.shape, mybir.dt.from_np(a.dtype), kind="ExternalInput").ap())
    out = nc.dram_tensor("out", inputs["x"].shape, mybir.dt.float32, kind="ExternalOutput").ap()
    gat_gcn_resnorm(nc, *args, out)
    r = run_bass_kernel_spmd(nc, [arrays], core_ids=[0])
    return r.results[0]["out"]
```
